# Optimizing a Trainium2 kernel written in Bass

```python
import numpy as np
import jax
import jax.numpy as jnp

def _softmax(x, axis=-1):
    return jax.nn.softmax(x, axis=axis)

def _gelu(x):
    return jax.nn.gelu(x, approximate=True)

def _silu(x):
    return jax.nn.silu(x)

def _sigmoid(x):
    return jax.nn.sigmoid(x)

def _layernorm(x, axis=-1, eps=1e-05):
    m = jnp.mean(x, axis=axis, keepdims=True)
    v = jnp.var(x, axis=axis, keepdims=True)
    return (x - m) / jnp.sqrt(v + eps)

def _scatter_add(tgt, idx, src, axis=0):
    return tgt.at[idx].add(src)

def _segment_sum(src, seg, n):
    return jax.ops.segment_sum(src, seg, n)
kernel_name = 'mk_macaron_d1_jaxref_r8_39bb2c'

def setup_inputs(seed: int=0):
    np.random.seed(seed)
    _w = jnp.asarray

    def _L0_attn_setup():
        import jax, jax.numpy as jnp
        import numpy as np
        CHUNK = 32
        ROPE_BASE = 10000.0
        EPS = 1e-06

        def _rmsnorm(x, scale):
            xf = x.astype(jnp.float32)
            rms = jax.lax.rsqrt(jnp.mean(xf * xf, axis=-1, keepdims=True) + EPS)
            out = scale.astype(jnp.float32) * (xf * rms)
            return jnp.clip(out, -60000.0, 60000.0).astype(x.dtype)

        def _rope(v, N, d_head, dtype):
            half = d_head // 2
            inv_freq = 1.0 / ROPE_BASE ** (jnp.arange(0, d_head, 2, dtype=jnp.float32) / d_head)
            freqs = jnp.arange(N, dtype=jnp.float32)[:, None] * inv_freq[None, :]
            cos = jnp.cos(freqs).astype(dtype)[None, :, None, :]
            sin = jnp.sin(freqs).astype(dtype)[None, :, None, :]
            v1, v2 = (v[..., :half], v[..., half:])
            return jnp.concatenate([v1 * cos - v2 * sin, v1 * sin + v2 * cos], axis=-1)
        key = jax.random.key(seed)
        ks = jax.random.split(key, 8)
        B, N, D, H, K = (4, 1024, 128, 16, 4)
        x = jax.random.normal(ks[0], (B, N, D), dtype=jnp.float32)
        norm_scale = jnp.ones((D,), dtype=jnp.float32)
        conv_w = jax.random.normal(ks[1], (D, 1, K), dtype=jnp.float32) * 0.2
        conv_b = jax.random.normal(ks[2], (D,), dtype=jnp.float32) * 0.02
        in_proj_w = jax.random.normal(ks[3], (D, 3 * D), dtype=jnp.float32) * 0.02
        dt_bias = jax.random.normal(ks[4], (D,), dtype=jnp.float32) * 0.5
        head_mix = jnp.eye(H, dtype=jnp.float32) + 0.02 * jax.random.normal(ks[5], (H, H), dtype=jnp.float32)
        out_proj_w = jax.random.normal(ks[6], (D, D), dtype=jnp.float32) * 0.02
        return {'x': x, 'norm_scale': norm_scale, 'conv_w': conv_w, 'conv_b': conv_b, 'in_proj_w': in_proj_w, 'dt_bias': dt_bias, 'head_mix': head_mix, 'out_proj_w': out_proj_w}
    _L0_attn_in = _L0_attn_setup()

    def _L0_ffn_setup():
        import jax, jax.numpy as jnp
        import numpy as np
        B, T, H = (8, 256, 128)
        F = 512
        E = 8
        TOP_K = 2
        key = jax.random.key(seed)
        ks = jax.random.split(key, 6)
        s_h = 1.0 / np.sqrt(H)
        s_f = 1.0 / np.sqrt(F)
        return {'hidden_states': jax.random.normal(ks[0], (B, T, H), dtype=jnp.float32), 'gate_w': jax.random.uniform(ks[1], (H, E), minval=-s_h, maxval=s_h, dtype=jnp.float32), 'w1': jax.random.uniform(ks[2], (E, H, F), minval=-s_h, maxval=s_h, dtype=jnp.float32), 'b1': jax.random.uniform(ks[3], (E, F), minval=-s_h, maxval=s_h, dtype=jnp.float32), 'w2': jax.random.uniform(ks[4], (E, F, H), minval=-s_f, maxval=s_f, dtype=jnp.float32), 'b2': jax.random.uniform(ks[5], (E, H), minval=-s_f, maxval=s_f, dtype=jnp.float32)}
    _L0_ffn_in = _L0_ffn_setup()
    _d = {'L0_attn_x': _L0_attn_in['x'], 'L0_attn_norm_scale': _L0_attn_in['norm_scale'], 'L0_attn_conv_w': _L0_attn_in['conv_w'], 'L0_attn_conv_b': _L0_attn_in['conv_b'], 'L0_attn_in_proj_w': _L0_attn_in['in_proj_w'], 'L0_attn_dt_bias': _L0_attn_in['dt_bias'], 'L0_attn_head_mix': _L0_attn_in['head_mix'], 'L0_attn_out_proj_w': _L0_attn_in['out_proj_w'], 'L0_ffn_gate_w': _L0_ffn_in['gate_w'], 'L0_ffn_w1': _L0_ffn_in['w1'], 'L0_ffn_b1': _L0_ffn_in['b1'], 'L0_ffn_w2': _L0_ffn_in['w2'], 'L0_ffn_b2': _L0_ffn_in['b2']}
    _x0 = _d['L0_attn_x']
    _d['L0_attn_x'] = jax.random.normal(jax.random.fold_in(jax.random.key(seed), 1), (4, 1024, 128), dtype=_x0.dtype)
    del _x0
    return _d

def reference(L0_attn_x, L0_attn_norm_scale, L0_attn_conv_w, L0_attn_conv_b, L0_attn_in_proj_w, L0_attn_dt_bias, L0_attn_head_mix, L0_attn_out_proj_w, L0_ffn_gate_w, L0_ffn_w1, L0_ffn_b1, L0_ffn_w2, L0_ffn_b2):

    def _L0_attn_ref(x, norm_scale, conv_w, conv_b, in_proj_w, dt_bias, head_mix, out_proj_w):
        import jax, jax.numpy as jnp
        import numpy as np
        CHUNK = 32
        ROPE_BASE = 10000.0
        EPS = 1e-06

        def _rmsnorm(x, scale):
            xf = x.astype(jnp.float32)
            rms = jax.lax.rsqrt(jnp.mean(xf * xf, axis=-1, keepdims=True) + EPS)
            out = scale.astype(jnp.float32) * (xf * rms)
            return jnp.clip(out, -60000.0, 60000.0).astype(x.dtype)

        def _rope(v, N, d_head, dtype):
            half = d_head // 2
            inv_freq = 1.0 / ROPE_BASE ** (jnp.arange(0, d_head, 2, dtype=jnp.float32) / d_head)
            freqs = jnp.arange(N, dtype=jnp.float32)[:, None] * inv_freq[None, :]
            cos = jnp.cos(freqs).astype(dtype)[None, :, None, :]
            sin = jnp.sin(freqs).astype(dtype)[None, :, None, :]
            v1, v2 = (v[..., :half], v[..., half:])
            return jnp.concatenate([v1 * cos - v2 * sin, v1 * sin + v2 * cos], axis=-1)
        residual = x
        B, N, D = x.shape
        H = head_mix.shape[0]
        d_head = D // H
        xn = _rmsnorm(x, norm_scale)
        K = conv_w.shape[-1]
        xc = jax.lax.conv_general_dilated(xn.transpose(0, 2, 1), conv_w, window_strides=(1,), padding=[(K - 1, 0)], feature_group_count=D, dimension_numbers=('NCH', 'OIH', 'NCH'))
        xc = (xc + conv_b[None, :, None]).transpose(0, 2, 1)
        xc = xc * jax.nn.sigmoid(xc)
        fused = xc @ in_proj_w
        dt_raw, v, gate_raw = jnp.split(fused, 3, axis=-1)
        dt = jnp.clip(jax.nn.softplus(dt_raw.astype(jnp.float32) + dt_bias.astype(jnp.float32)), 0.001, 2.0).astype(dt_raw.dtype)
        gate = jax.nn.sigmoid(gate_raw)
        log_alpha = -dt.astype(jnp.float32)
        v_rot = _rope(v.reshape(B, N, H, d_head), N, d_head, x.dtype).reshape(B, N, D)
        v_in = (v_rot * dt).astype(jnp.float32)
        pad = -N % CHUNK
        if pad:
            v_in = jnp.pad(v_in, ((0, 0), (0, pad), (0, 0)))
            log_alpha = jnp.pad(log_alpha, ((0, 0), (0, pad), (0, 0)))
        Np = N + pad
        nc = Np // CHUNK
        v_ch = v_in.reshape(B, nc, CHUNK, D)
        la_ch = log_alpha.reshape(B, nc, CHUNK, D)
        L = jnp.clip(jnp.cumsum(la_ch, axis=2), -20.0, 0.0)
        L_max = jnp.max(L, axis=2, keepdims=True)
        L_st = L - L_max
        cum_scaled = jnp.cumsum(jnp.exp(-L_st) * v_ch, axis=2)
        chunk_out = jnp.exp(L_st) * cum_scaled
        if nc > 1:
            bdecay = L[:, :, -1, :]
            bout = chunk_out[:, :, -1, :]
            cum_decay = jnp.clip(jnp.cumsum(bdecay, axis=1), -80.0, 0.0)
            stab = jnp.max(cum_decay, axis=1, keepdims=True)
            ncd = jnp.clip(cum_decay - stab, -20.0, 0.0)
            seeds = bout * jnp.exp(-ncd)
            shifted = jnp.pad(seeds[:, :-1], ((0, 0), (1, 0), (0, 0)))
            carries = jnp.cumsum(shifted, axis=1) * jnp.exp(ncd)
            final = chunk_out + carries[:, :, None, :] * jnp.exp(L)
        else:
            final = chunk_out
        final = final.astype(x.dtype).reshape(B, Np, D)[:, :N, :]
        v_mix = jnp.einsum('bnhd,hm->bnmd', final.reshape(B, N, H, d_head), head_mix)
        final = v_mix.reshape(B, N, D)
        out = final * gate @ out_proj_w
        return residual + out

    def _L0_ffn_ref(hidden_states, gate_w, w1, b1, w2, b2):
        import jax, jax.numpy as jnp
        import numpy as np
        B, T, H = (8, 256, 128)
        F = 512
        E = 8
        TOP_K = 2
        b, t, h = hidden_states.shape
        seq_rep = hidden_states.mean(axis=1)
        router_logits = seq_rep @ gate_w
        probs = jax.nn.softmax(router_logits.astype(jnp.float32), axis=-1)
        top_w, top_i = jax.lax.top_k(probs, TOP_K)
        top_w = top_w / top_w.sum(axis=-1, keepdims=True)
        top_w = top_w.astype(hidden_states.dtype)
        combine = jnp.zeros((b, E), dtype=hidden_states.dtype)
        combine = combine.at[jnp.arange(b)[:, None], top_i].set(top_w)
        out = jnp.zeros_like(hidden_states)
        for e in range(E):
            hmid = jax.nn.gelu(jnp.einsum('bth,hf->btf', hidden_states, w1[e]) + b1[e], approximate=False)
            y = jnp.einsum('btf,fh->bth', hmid, w2[e]) + b2[e]
            out = out + combine[:, e][:, None, None] * y
        return out
    x = L0_attn_x
    x = x + 0.5 * _L0_ffn_ref(_layernorm(x, axis=-1), L0_ffn_gate_w, L0_ffn_w1, L0_ffn_b1, L0_ffn_w2, L0_ffn_b2)
    x = x + _L0_attn_ref(_layernorm(x, axis=-1), L0_attn_norm_scale, L0_attn_conv_w, L0_attn_conv_b, L0_attn_in_proj_w, L0_attn_dt_bias, L0_attn_head_mix, L0_attn_out_proj_w)
    x = x + 0.5 * _L0_ffn_ref(_layernorm(x, axis=-1), L0_ffn_gate_w, L0_ffn_w1, L0_ffn_b1, L0_ffn_w2, L0_ffn_b2)
    return x

_drawn_inputs = setup_inputs


def setup_inputs(seed=0):
    import zlib

    import numpy as np

    out = dict(_drawn_inputs(seed))
    spreads = {'L0_attn_norm_scale': (1.0, 0.6)}
    factors = {'L0_attn_conv_w': 8.0,
     'L0_attn_conv_b': 8.0,
     'L0_attn_in_proj_w': 8.0,
     'L0_attn_dt_bias': 8.0,
     'L0_attn_head_mix': 8.0,
     'L0_attn_out_proj_w': 8.0,
     'L0_ffn_b1': 2.847}
    for name, (base, spread) in spreads.items():
        noise = np.random.default_rng([zlib.crc32(name.encode()), seed]).standard_normal(out[name].shape)
        drawn = base * np.exp(spread * noise) if base else spread * noise
        out[name] = jnp.asarray(drawn.astype(out[name].dtype))
    for name, factor in factors.items():
        out[name] = (out[name] * factor).astype(out[name].dtype)
    return out
```

```python
from contextlib import ExitStack

import concourse.bass as bass
from concourse import mybir

ALU = mybir.AluOpType
ACT = mybir.ActivationFunctionType
F32 = mybir.dt.float32
U32 = mybir.dt.uint32
AX_X = mybir.AxisListType.X

P = 128
HALF = 512
CHUNK = 32
LN_EPS, RMS_EPS = 1e-5, 1e-6
XN_MAX = 60000.0
DT_MIN, DT_MAX = 0.001, 2.0
DECAY_MAX, CUM_DECAY_MAX = 20.0, 80.0

LAG = 1
POST = 1
MIX_NORM = 4
MIX_DT, MIX_V, MIX_VS, MIX_GATE = 7, 8, 9, 10
MIX_HEADS = 12
MIX_OUT = 14
PRE_NORM, PRE_ROUTE = 2, 3


def macaron_kernel(nc, x, wpack, gate_w, proj, vecs, rope, out):
    B, N, D = x.shape
    E = gate_w.shape[1]
    F = (wpack.shape[2] - 1) // (2 + 1 / P)
    F = int(round(F))
    FT = F // P
    NT = N // P
    NCH = N // CHUNK
    TOP = 2
    SLOTS = TOP * FT
    PASSES = 2 * B
    PACK = wpack.shape[2]
    W2_AT, B1_AT, B2_AT = F, 2 * F, 2 * F + FT
    HBUF = 4
    assert D == P and N == 2 * HALF and PACK == 2 * F + FT + 1
    H = vecs.shape[1] - 4 - 3
    DH = D // H

    with ExitStack() as ctx:
        def sb(name, shape, dt=F32):
            return ctx.enter_context(nc.sbuf_tensor(name, shape, dt))

        def sem(name):
            return ctx.enter_context(nc.semaphore(name))

        hid_ps = ctx.enter_context(nc.psum_tensor("hid_ps", [P, 2, N], F32))
        y_ps = ctx.enter_context(nc.psum_tensor("y_ps", [P, N], F32))
        aux_ps = ctx.enter_context(nc.psum_tensor("aux_ps", [P, N], F32))

        xt = sb("xt", [P, B, NT, D])
        ident = sb("ident", [P, P])
        ones = sb("ones", [P, P])
        neg_half = sb("neg_half", [P, NT])
        gate_sb = sb("gate_sb", [P, E])
        proj_sb = sb("proj_sb", [P, 5, P])
        vec_sb = sb("vec_sb", [P, 7 + H])
        conv_w, conv_b = vec_sb[:, 0:4], vec_sb[:, 4:5]
        dt_bias, norm_scale, mix_col = vec_sb[:, 5:6], vec_sb[:, 6:7], vec_sb[:, 7:7 + H]
        rope_sb = sb("rope_sb", [P, 2, N])
        head_eye = sb("head_eye", [P, DH])
        mix_sb = sb("mix_sb", [P, H, DH])
        in_chunk = sb("in_chunk", [P, N])
        cum_cap = sb("cum_cap", [P, NCH])
        w_sb = sb("w_sb", [P, 2, TOP, PACK])
        f_stat = sb("f_stat", [P, NT, 6])
        f_mv = sb("f_mv", [P, NT, 2])
        f_ve = sb("f_ve", [P, NT])
        f_rstd = sb("f_rstd", [P, NT])
        f_tok = sb("f_tok", [P, NT, D])
        zt = sb("zt", [P, 2, N])
        zsum = sb("zsum", [P, 1])
        zsum_wide = sb("zsum_wide", [P, P])
        logit = sb("logit", [P, E])
        top_v = sb("top_v", [P, 8])
        top_i = sb("top_i", [P, 8], U32)
        top_d = sb("top_d", [P, 1])
        top_t = sb("top_t", [P, 1])
        coef = sb("coef", [P, 2, TOP])
        bias2a = sb("bias2a", [P, 1])
        bias2 = sb("bias2", [P, 2, 1])
        hid = sb("hid", [P, HBUF, N])
        yt = sb("yt", [P, N])
        m_stat = sb("m_stat", [P, NT, 6])
        m_mv = sb("m_mv", [P, NT, 2])
        m_ve = sb("m_ve", [P, NT])
        m_rstd = sb("m_rstd", [P, NT])
        m_sq = sb("m_sq", [P, NT])
        m_ms = sb("m_ms", [P, NT])
        m_rms = sb("m_rms", [P, NT])
        m_h = sb("m_h", [P, NT, D])
        m_tok = sb("m_tok", [P, NT, D])
        PAD = 3
        xs = sb("xs", [P, PAD + N])
        xc = sb("xc", [P, N])
        xc_tanh = sb("xc_tanh", [P, N])
        silu = sb("silu", [P, N])
        dt_e = sb("dt_e", [P, N])
        dt_raw = sb("dt_raw", [P, N])
        dt_t = sb("dt_t", [P, N])
        decay = sb("decay", [P, N])
        dstep = sb("dstep", [P, N])
        alpha = sb("alpha", [P, N])
        small = sb("small", [P, 2, NCH])
        small_e = sb("small_e", [P, 2, NCH])
        cumd = sb("cumd", [P, NCH])
        ncd = sb("ncd", [P, NCH])
        carry = sb("carry", [P, NCH])
        carry_p = sb("carry_p", [P, NCH])
        va = sb("va", [P, N])
        vb = sb("vb", [P, N])
        vr = sb("vr", [P, N])
        u = sb("u", [P, N])
        local = sb("local", [P, N])
        final = sb("final", [P, N])
        gate_t = sb("gate_t", [P, N])
        gated = sb("gated", [P, N])

        def first_of(t):
            return t[:, :].rearrange("p (c t) -> p c t", t=CHUNK)[:, :, 0]

        def last_of(t):
            return t[:, :].rearrange("p (c t) -> p c t", t=CHUNK)[:, :, CHUNK - 1]

        x_in = [sem(f"x_in{b}") for b in range(B)]
        proj_in, rope_in, small_in = sem("proj_in"), sem("rope_in"), sem("small_in")
        w_in = [sem(f"w_in{i}") for i in range(2)]
        out_done = sem("out_done")
        made_ident, made_const, made_proj, made_mix = (
            sem("made_ident"), sem("made_const"), sem("made_proj"), sem("made_mix"))
        f_stats_step, f_aggr_done = sem("f_stats_step"), sem("f_aggr_done")
        f_var_eps, f_rstd_done, f_norm_done = sem("f_var_eps"), sem("f_rstd_done"), sem("f_norm_done")
        f_turned, zt_ready, zsum_ready, zwide_ready = (
            sem("f_turned"), sem("zt_ready"), sem("zsum_ready"), sem("zwide_ready"))
        logits_up, logits_read, top_ready = sem("logits_up"), sem("logits_read"), sem("top_ready")
        index_ready, diff_ready, tanh_ready, coef_ready = (
            sem("index_ready"), sem("diff_ready"), sem("tanh_ready"), sem("coef_ready"))
        bias2a_ready, bias2_ready, w2_scaled = sem("bias2a_ready"), sem("bias2_ready"), sem("w2_scaled")
        hid_up, hid_ready, hid_used = sem("hid_up"), sem("hid_ready"), sem("hid_used")
        yt_ready, y_turned, x_updated = sem("yt_ready"), sem("y_turned"), sem("x_updated")
        m_stats_step, m_aggr_done, m_pool_step = sem("m_stats_step"), sem("m_aggr_done"), sem("m_pool_step")
        m_h_done, m_norm_done, x_plus_h = sem("m_h_done"), sem("m_norm_done"), sem("x_plus_h")
        m_turned, xs_ready, xs_clipped, conv_step = (
            sem("m_turned"), sem("xs_ready"), sem("xs_clipped"), sem("conv_step"))
        silu_tanh, silu_done = sem("silu_tanh"), sem("silu_done")
        dt_up, dt_exp, dt_ln, dt_done = sem("dt_up"), sem("dt_exp"), sem("dt_ln"), sem("dt_done")
        decay_sum, decay_done, dstep_done, first_done = (
            sem("decay_sum"), sem("decay_done"), sem("dstep_done"), sem("first_done"))
        cumd_done, ncd_done, small_done = sem("cumd_done"), sem("ncd_done"), sem("small_done")
        alpha_exp, small_exp, alpha_done = sem("alpha_exp"), sem("small_exp"), sem("alpha_done")
        v_up, v_cos, vs_up, v_sin, v_rot, u_ready = (
            sem("v_up"), sem("v_cos"), sem("vs_up"), sem("v_sin"), sem("v_rot"), sem("u_ready"))
        local_done, carry_done, carry_scaled, u_seeded, final_done = (
            sem("local_done"), sem("carry_done"), sem("carry_scaled"), sem("u_seeded"), sem("final_done"))
        gate_up, gate_tanh, heads_up, gated_done, out_up, x_mixed = (
            sem("gate_up"), sem("gate_tanh"), sem("heads_up"), sem("gated_done"), sem("out_up"), sem("x_mixed"))

        LAST = PASSES * SLOTS + LAG + POST + 1

        def after_pass(slot, offset):
            q, r = divmod(slot - offset, SLOTS)
            return [q - 1] if r == 0 and 1 <= q <= PASSES else []

        def mixer_at(slot, offset):
            return [b for b in after_pass(slot, offset) if b < B]

        def before_pass(slot, offset):
            q, r = divmod(slot - offset, SLOTS)
            return [q + 1] if r == 0 and 0 <= q < PASSES - 1 else []

        block = ctx.enter_context(nc.Block())

        @block.sync
        def _(sp):
            def load_x(b):
                sp.dma_start(xt[:, b, :, :], x[b].rearrange("(t p) d -> p t d", p=P)).then_inc(x_in[b], 16)

            def load_experts(q):
                if q >= 2:
                    sp.wait_ge(hid_used, SLOTS * (q - 1))
                    sp.wait_ge(bias2_ready, q - 1)
                sp.wait_ge(index_ready, q + 1)
                for k in range(TOP):
                    e = sp.value_load(top_i[0:1, k:k + 1], min_val=0, max_val=E - 1)
                    src = wpack[bass.ds(e, 1), :, :].rearrange("e p n -> p (e n)")
                    sp.dma_start(w_sb[:, q % 2, k, :], src).then_inc(w_in[q % 2], 16)

            load_x(0)
            sp.dma_start(gate_sb[:, :], gate_w).then_inc(small_in, 16)
            sp.dma_start(vec_sb[:, :], vecs).then_inc(small_in, 16)
            load_x(1)
            load_experts(0)
            load_x(2)
            load_x(3)
            for slot in range(LAST):
                for q in after_pass(slot, POST + 1):
                    if q >= B:
                        sp.wait_ge(x_updated, q + 1)
                        sp.dma_start(out[q - B].rearrange("(t p) d -> p t d", p=P),
                                     xt[:, q - B, :, :]).then_inc(out_done, 16)
                for q in before_pass(slot, PRE_ROUTE):
                    load_experts(q)
            sp.wait_ge(out_done, 16 * B)

        @block.gpsimd
        def _(pool):
            pool.dma_start(proj_sb[:, :, :], proj.rearrange("p (k n) -> p k n", n=P)).then_inc(proj_in, 16)
            pool.dma_start(rope_sb[:, :, :], rope.rearrange("k p n -> p k n")).then_inc(rope_in, 16)
            nc.gpsimd.memset(ident[:, :], 0.0).then_inc(made_ident, 1)
            pool.wait_ge(made_ident, 1)
            nc.gpsimd.affine_select(out=ident[:, :], in_=ident[:, :], compare_op=ALU.not_equal, fill=1.0,
                                    base=0, pattern=[[-1, P]], channel_multiplier=1).then_inc(made_ident, 1)
            nc.gpsimd.memset(neg_half[:, :], -0.5).then_inc(made_const, 1)
            nc.gpsimd.memset(ones[:, :], 1.0).then_inc(made_const, 1)
            nc.gpsimd.memset(xs[:, 0:PAD], 0.0).then_inc(made_const, 1)
            nc.gpsimd.memset(dstep[:, 0:1], 0.0).then_inc(made_const, 1)
            nc.gpsimd.memset(small[:, 1, 0:1], 0.0).then_inc(made_const, 1)
            nc.gpsimd.memset(cum_cap[:, :], CUM_DECAY_MAX).then_inc(made_const, 1)

            def pass_rstd(q):
                pool.wait_ge(f_aggr_done, NT * (q + 1))
                if q:
                    pool.wait_ge(f_norm_done, NT * q)
                nc.gpsimd.tensor_scalar(f_ve[:, :], f_mv[:, :, 1], LN_EPS, None, ALU.add).then_inc(f_var_eps, 1)
                pool.wait_ge(f_var_eps, q + 1)
                nc.gpsimd.tensor_tensor(f_rstd[:, :], f_ve[:, :], neg_half[:, :], ALU.pow).then_inc(f_rstd_done, 1)

            def scale_w2(q):
                pool.wait_ge(w_in[q % 2], 16 * TOP * (q // 2 + 1))
                pool.wait_ge(coef_ready, TOP * (q + 1))
                for k in range(TOP):
                    w2 = w_sb[:, q % 2, k, W2_AT:W2_AT + F]
                    nc.gpsimd.tensor_scalar(w2, w2, coef[:, q % 2, k:k + 1], None, ALU.mult).then_inc(w2_scaled, 1)

            STEPS = 6

            def mixer_rms(b):
                n = STEPS * b
                pool.wait_ge(m_aggr_done, NT * (b + 1))
                if b:
                    pool.wait_ge(m_norm_done, NT * b)
                nc.gpsimd.tensor_scalar(m_ve[:, :], m_mv[:, :, 1], LN_EPS, None, ALU.add).then_inc(m_pool_step, 1)
                pool.wait_ge(m_pool_step, n + 1)
                nc.gpsimd.tensor_tensor(m_rstd[:, :], m_ve[:, :], neg_half[:, :], ALU.pow).then_inc(m_pool_step, 1)
                pool.wait_ge(m_pool_step, n + 2)
                nc.gpsimd.tensor_tensor(m_sq[:, :], m_rstd[:, :], m_rstd[:, :], ALU.mult).then_inc(m_pool_step, 1)
                pool.wait_ge(m_pool_step, n + 3)
                nc.gpsimd.tensor_tensor(m_ms[:, :], m_sq[:, :], m_mv[:, :, 1], ALU.mult).then_inc(m_pool_step, 1)
                pool.wait_ge(m_pool_step, n + 4)
                nc.gpsimd.tensor_scalar(m_ms[:, :], m_ms[:, :], RMS_EPS, None, ALU.add).then_inc(m_pool_step, 1)
                pool.wait_ge(m_pool_step, n + 5)
                nc.gpsimd.tensor_tensor(m_rms[:, :], m_ms[:, :], neg_half[:, :], ALU.pow).then_inc(m_pool_step, 1)

            def mixer_residual(b):
                pool.wait_ge(m_h_done, NT * (b + 1))
                xb = xt[:, b, :, :]
                nc.gpsimd.tensor_tensor(xb, xb, m_h[:, :, :], ALU.add).then_inc(x_plus_h, 1)

            def mixer_input(b):
                pool.wait_ge(v_cos, b + 1)
                pool.wait_ge(v_sin, b + 1)
                if b:
                    pool.wait_ge(final_done, b)
                nc.gpsimd.tensor_tensor(vr[:, :], va[:, :], vb[:, :], ALU.add).then_inc(v_rot, 1)
                pool.wait_ge(v_rot, b + 1)
                pool.wait_ge(dt_done, b + 1)
                nc.gpsimd.tensor_tensor(u[:, :], vr[:, :], dt_t[:, :], ALU.mult).then_inc(u_ready, 1)

            pool.wait_ge(made_const, 2)
            pass_rstd(0)
            nc.gpsimd.memset(in_chunk[:, :], 1.0).then_inc(made_const, 1)
            pool.wait_ge(made_const, 7)
            nc.gpsimd.memset(first_of(in_chunk), 0.0).then_inc(made_const, 1)
            scale_w2(0)
            for slot in range(LAST):
                for q in before_pass(slot, PRE_NORM - 1):
                    pass_rstd(q)
                for b in mixer_at(slot, POST):
                    mixer_rms(b)
                for b in mixer_at(slot, POST + 1):
                    mixer_residual(b)
                for q in before_pass(slot, PRE_ROUTE + 2):
                    scale_w2(q)
                for b in mixer_at(slot, MIX_VS):
                    mixer_input(b)

        @block.scalar
        def _(act):
            def turn_z(q):
                act.wait_ge(f_turned, q + 1)
                if q >= 2:
                    act.wait_ge(hid_up, SLOTS * (q - 1))
                if q:
                    act.wait_ge(zwide_ready, q)
                nc.scalar.activation(zt[:, q % 2, :], aux_ps[:, :], ACT.Copy,
                                     accum_out=zsum[:, :]).then_inc(zt_ready, 1)

            def top_tanh(q):
                act.wait_ge(diff_ready, q + 1)
                nc.scalar.activation(top_t[:, :], top_d[:, :], ACT.Tanh, scale=0.5 / N).then_inc(tanh_ready, 1)

            def gelu(slot):
                q, t = divmod(slot, SLOTS)
                act.wait_ge(hid_up, slot + 1)
                if slot >= HBUF:
                    act.wait_ge(hid_used, slot - HBUF + 1)
                if t == 0:
                    act.wait_ge(w_in[q % 2], 16 * TOP * (q // 2 + 1))
                k, f = divmod(t, FT)
                bias = w_sb[:, q % 2, k, B1_AT + f:B1_AT + f + 1]
                nc.scalar.activation(hid[:, slot % HBUF, :], hid_ps[:, slot % 2, :], ACT.Gelu,
                                     bias=bias).then_inc(hid_ready, 1)

            def pass_out(q):
                act.wait_ge(hid_used, SLOTS * (q + 1))
                act.wait_ge(bias2_ready, q + 1)
                if q:
                    act.wait_ge(y_turned, q)
                nc.scalar.activation(yt[:, :], y_ps[:, :], ACT.Identity,
                                     bias=bias2[:, q % 2, :]).then_inc(yt_ready, 1)

            def mixer_scale(b):
                act.wait_ge(m_turned, b + 1)
                if b:
                    act.wait_ge(conv_step, 4 * b)
                nc.scalar.activation(xs[:, PAD:], aux_ps[:, :], ACT.Copy, scale=norm_scale).then_inc(xs_ready, 1)

            def mixer_silu(b):
                act.wait_ge(conv_step, 4 * (b + 1))
                if b:
                    act.wait_ge(silu_done, b)
                nc.scalar.activation(xc_tanh[:, :], xc[:, :], ACT.Tanh, scale=0.5).then_inc(silu_tanh, 1)

            def mixer_dt(b):
                act.wait_ge(dt_up, b + 1)
                if b:
                    act.wait_ge(dt_done, b)
                nc.scalar.preload_act_table_set("natural_log_exp_and_others")
                nc.scalar.activation(dt_e[:, :], aux_ps[:, :], ACT.Exp, bias=dt_bias).then_inc(dt_exp, 1)
                act.wait_ge(dt_exp, b + 1)
                nc.scalar.activation(dt_raw[:, :], dt_e[:, :], ACT.Ln, bias=1.0).then_inc(dt_ln, 1)

            def mixer_decay(b):
                act.wait_ge(dstep_done, b + 1)
                if b:
                    act.wait_ge(final_done, b)
                nc.scalar.preload_act_table_set("natural_log_exp_and_others")
                nc.scalar.activation(alpha[:, :], dstep[:, :], ACT.Exp).then_inc(alpha_exp, 1)
                act.wait_ge(small_done, b + 1)
                nc.scalar.activation(small_e[:, :, :], small[:, :, :], ACT.Exp).then_inc(small_exp, 1)

            def mixer_gate(b):
                act.wait_ge(gate_up, b + 1)
                if b:
                    act.wait_ge(gated_done, b)
                nc.scalar.activation(gate_t[:, :], aux_ps[:, :], ACT.Tanh, scale=0.5).then_inc(gate_tanh, 1)

            act.wait_ge(small_in, 32)
            act.wait_ge(made_const, 6)
            turn_z(0)
            top_tanh(0)
            for slot in range(LAST):
                for b in mixer_at(slot, MIX_DT):
                    mixer_silu(b)
                if slot < PASSES * SLOTS:
                    gelu(slot)
                for q in after_pass(slot, POST - 1):
                    pass_out(q)
                for q in before_pass(slot, PRE_NORM):
                    turn_z(q)
                for q in before_pass(slot, PRE_ROUTE):
                    top_tanh(q)
                for b in mixer_at(slot, MIX_NORM):
                    mixer_scale(b)
                for b in mixer_at(slot, MIX_DT):
                    mixer_dt(b)
                for b in mixer_at(slot, MIX_V + 1):
                    mixer_decay(b)
                for b in mixer_at(slot, MIX_GATE):
                    mixer_gate(b)

        @block.tensor
        def _(pe):
            def up(slot):
                q, t = divmod(slot, SLOTS)
                k, f = divmod(t, FT)
                if t == 0:
                    pe.wait_ge(w_in[q % 2], 16 * TOP * (q // 2 + 1))
                    pe.wait_ge(zt_ready, q + 1)
                if slot >= 2:
                    pe.wait_ge(hid_ready, slot - 1)
                w1 = w_sb[:, q % 2, k, f * P:(f + 1) * P]
                for h in range(2):
                    cols = slice(h * HALF, (h + 1) * HALF)
                    last = nc.tensor.matmul(hid_ps[:, slot % 2, cols], w1, zt[:, q % 2, cols],
                                            start=True, stop=True)
                last.then_inc(hid_up, 1)

            def down(slot):
                q, t = divmod(slot, SLOTS)
                k, f = divmod(t, FT)
                pe.wait_ge(hid_ready, slot + 1)
                if t == 0:
                    pe.wait_ge(w2_scaled, TOP * (q + 1))
                    if q:
                        pe.wait_ge(yt_ready, q)
                w2 = w_sb[:, q % 2, k, W2_AT + f * P:W2_AT + (f + 1) * P]
                for h in range(2):
                    cols = slice(h * HALF, (h + 1) * HALF)
                    last = nc.tensor.matmul(y_ps[:, cols], w2, hid[:, slot % HBUF, cols],
                                            start=t == 0, stop=t == SLOTS - 1)
                last.then_inc(hid_used, 1)

            reader = []

            def take_aux(*next_reader):
                if reader:
                    pe.wait_ge(*reader.pop())
                reader.append(next_reader)

            def turn(tiles):
                for t in range(NT):
                    last = nc.tensor.transpose(aux_ps[:, t * P:(t + 1) * P], tiles(t), ident[:, :])
                return last

            def project(w, src):
                for h in range(2):
                    cols = slice(h * HALF, (h + 1) * HALF)
                    last = nc.tensor.matmul(aux_ps[:, cols], w, src[:, cols], start=True, stop=True)
                return last

            def pre_norm(q):
                pe.wait_ge(f_norm_done, NT * (q + 1))
                take_aux(zt_ready, q + 1)
                turn(lambda t: f_tok[:, t, :]).then_inc(f_turned, 1)

            def pre_route(q):
                pe.wait_ge(zwide_ready, q + 1)
                take_aux(logits_read, q + 1)
                nc.tensor.matmul(aux_ps[:, 0:E], zsum_wide[:, :], gate_sb[:, :],
                                 start=True, stop=True).then_inc(logits_up, 1)

            def post(q):
                pe.wait_ge(yt_ready, q + 1)
                take_aux(x_updated, q + 1)
                turn(lambda t: yt[:, t * P:(t + 1) * P]).then_inc(y_turned, 1)

            def mixer_norm(b):
                pe.wait_ge(m_norm_done, NT * (b + 1))
                take_aux(xs_ready, b + 1)
                turn(lambda t: m_tok[:, t, :]).then_inc(m_turned, 1)

            def mixer_dt(b):
                pe.wait_ge(silu_done, b + 1)
                take_aux(dt_exp, b + 1)
                project(proj_sb[:, 0, :], silu).then_inc(dt_up, 1)

            def mixer_v(b):
                take_aux(v_cos, b + 1)
                project(proj_sb[:, 1, :], silu).then_inc(v_up, 1)

            def mixer_vs(b):
                take_aux(v_sin, b + 1)
                project(proj_sb[:, 2, :], silu).then_inc(vs_up, 1)

            def mixer_gate(b):
                take_aux(gate_tanh, b + 1)
                project(proj_sb[:, 3, :], silu).then_inc(gate_up, 1)

            def mixer_heads(b):
                pe.wait_ge(final_done, b + 1)
                take_aux(gated_done, b + 1)
                project(mix_sb[:, :, :].rearrange("p m d -> p (m d)"), final).then_inc(heads_up, 1)

            def mixer_out(b):
                pe.wait_ge(gated_done, b + 1)
                take_aux(x_mixed, b + 1)
                for t in range(NT):
                    cols = slice(t * P, (t + 1) * P)
                    last = nc.tensor.matmul(aux_ps[:, cols], gated[:, cols], proj_sb[:, 4, :],
                                            start=True, stop=True)
                last.then_inc(out_up, 1)

            pe.wait_ge(made_ident, 2)
            pre_norm(0)
            pe.wait_ge(small_in, 32)
            pre_route(0)
            pe.wait_ge(made_proj, 1)
            pe.wait_ge(made_mix, H)
            for slot in range(LAST):
                if slot < PASSES * SLOTS:
                    up(slot)
                if LAG <= slot < PASSES * SLOTS + LAG:
                    down(slot - LAG)
                for q in after_pass(slot, POST):
                    post(q)
                for q in before_pass(slot, PRE_NORM):
                    pre_norm(q)
                for q in before_pass(slot, PRE_ROUTE):
                    pre_route(q)
                for b in mixer_at(slot, MIX_NORM):
                    mixer_norm(b)
                for b in mixer_at(slot, MIX_DT):
                    mixer_dt(b)
                for b in mixer_at(slot, MIX_V):
                    mixer_v(b)
                for b in mixer_at(slot, MIX_VS):
                    mixer_vs(b)
                for b in mixer_at(slot, MIX_GATE):
                    mixer_gate(b)
                for b in mixer_at(slot, MIX_HEADS):
                    mixer_heads(b)
                for b in mixer_at(slot, MIX_OUT):
                    mixer_out(b)

        @block.vector
        def _(dve):
            V = nc.vector

            def pass_stats(q):
                b = q % B
                if q < B:
                    dve.wait_ge(x_in[b], 16)
                else:
                    dve.wait_ge(x_mixed, b + 1)
                if q:
                    dve.wait_ge(f_rstd_done, q)
                for t in range(NT):
                    V.bn_stats(f_stat[:, t, :], xt[:, b, t, :]).then_inc(f_stats_step, 1)
                for t in range(NT):
                    dve.wait_ge(f_stats_step, NT * q + t + 1)
                    V.bn_aggr(f_mv[:, t, :], f_stat[:, t, :]).then_inc(f_aggr_done, 1)

            def pass_normalise(q):
                dve.wait_ge(f_rstd_done, q + 1)
                if q:
                    dve.wait_ge(f_turned, q)
                dve.wait_ge(f_aggr_done, NT * (q + 1))
                for t in range(NT):
                    V.tensor_scalar(f_tok[:, t, :], xt[:, q % B, t, :], f_mv[:, t, 0:1], f_rstd[:, t:t + 1],
                                    ALU.subtract, ALU.mult).then_inc(f_norm_done, 1)

            def widen_sum(q):
                dve.wait_ge(zt_ready, q + 1)
                if q:
                    dve.wait_ge(logits_up, q)
                V.tensor_scalar(zsum_wide[:, :], ones[:, :], zsum[:, 0:1], None, ALU.mult).then_inc(zwide_ready, 1)

            def route(q):
                dve.wait_ge(logits_up, q + 1)
                V.tensor_copy(logit[:, :], aux_ps[:, 0:E]).then_inc(logits_read, 1)
                dve.wait_ge(logits_read, q + 1)
                V.max(top_v[:, :], logit[:, :]).then_inc(top_ready, 1)
                dve.wait_ge(top_ready, q + 1)
                if q:
                    dve.wait_ge(w_in[(q - 1) % 2], 16 * TOP * ((q - 1) // 2 + 1))
                V.max_index(top_i[:, :], top_v[:, :], logit[:, :]).then_inc(index_ready, 1)
                if q:
                    dve.wait_ge(tanh_ready, q)
                V.tensor_tensor(top_d[:, :], top_v[:, 0:1], top_v[:, 1:2], ALU.subtract).then_inc(diff_ready, 1)

            def coefficients(q):
                dve.wait_ge(tanh_ready, q + 1)
                for k in range(TOP):
                    V.tensor_scalar(coef[:, q % 2, k:k + 1], top_t[:, :], 0.25 if k == 0 else -0.25, 0.25,
                                    ALU.mult, ALU.add).then_inc(coef_ready, 1)

            def out_bias(q):
                dve.wait_ge(w_in[q % 2], 16 * TOP * (q // 2 + 1))
                dve.wait_ge(coef_ready, TOP * (q + 1))
                b2 = [w_sb[:, q % 2, k, B2_AT:B2_AT + 1] for k in range(TOP)]
                V.tensor_scalar(bias2a[:, :], b2[0], coef[:, q % 2, 0:1], None, ALU.mult).then_inc(bias2a_ready, 1)
                dve.wait_ge(bias2a_ready, q + 1)
                V.scalar_tensor_tensor(bias2[:, q % 2, :], b2[1], coef[:, q % 2, 1:2], bias2a[:, :],
                                       ALU.mult, ALU.add).then_inc(bias2_ready, 1)

            def update_x(q):
                dve.wait_ge(y_turned, q + 1)
                xb = xt[:, q % B, :, :].rearrange("p t d -> p (t d)")
                V.tensor_tensor(xb, aux_ps[:, :], xb, ALU.add).then_inc(x_updated, 1)

            def mixer_stats(b):
                dve.wait_ge(x_updated, b + 1)
                for t in range(NT):
                    V.bn_stats(m_stat[:, t, :], xt[:, b, t, :]).then_inc(m_stats_step, 1)
                if b:
                    dve.wait_ge(m_pool_step, 6 * b)
                for t in range(NT):
                    dve.wait_ge(m_stats_step, NT * b + t + 1)
                    V.bn_aggr(m_mv[:, t, :], m_stat[:, t, :]).then_inc(m_aggr_done, 1)

            def mixer_normalise(b):
                dve.wait_ge(m_pool_step, 6 * b + 2)
                dve.wait_ge(m_aggr_done, NT * (b + 1))
                if b:
                    dve.wait_ge(x_plus_h, b)
                for t in range(NT):
                    V.tensor_scalar(m_h[:, t, :], xt[:, b, t, :], m_mv[:, t, 0:1], m_rstd[:, t:t + 1],
                                    ALU.subtract, ALU.mult).then_inc(m_h_done, 1)
                dve.wait_ge(m_pool_step, 6 * (b + 1))
                if b:
                    dve.wait_ge(m_turned, b)
                for t in range(NT):
                    dve.wait_ge(m_h_done, NT * b + t + 1)
                    V.tensor_scalar(m_tok[:, t, :], m_h[:, t, :], m_rms[:, t:t + 1], None,
                                    ALU.mult).then_inc(m_norm_done, 1)

            def mixer_conv(b):
                dve.wait_ge(xs_ready, b + 1)
                V.tensor_scalar(xs[:, PAD:], xs[:, PAD:], XN_MAX, -XN_MAX, ALU.min, ALU.max).then_inc(xs_clipped, 1)
                dve.wait_ge(xs_clipped, b + 1)
                V.tensor_scalar(xc[:, :], xs[:, 0:N], conv_w[:, 0:1], conv_b, ALU.mult, ALU.add).then_inc(conv_step, 1)
                for k in range(1, 4):
                    dve.wait_ge(conv_step, 4 * b + k)
                    V.scalar_tensor_tensor(xc[:, :], xs[:, k:k + N], conv_w[:, k:k + 1], xc[:, :],
                                           ALU.mult, ALU.add).then_inc(conv_step, 1)

            def mixer_silu(b):
                dve.wait_ge(silu_tanh, b + 1)
                if b:
                    dve.wait_ge(gate_up, b)
                V.scalar_tensor_tensor(silu[:, :], xc_tanh[:, :], 1.0, xc[:, :],
                                       ALU.add, ALU.mult).then_inc(silu_done, 1)

            def mixer_decay(b):
                dve.wait_ge(dt_ln, b + 1)
                if b:
                    dve.wait_ge(u_ready, b)
                V.tensor_scalar(dt_t[:, :], dt_raw[:, :], DT_MIN, DT_MAX, ALU.max, ALU.min).then_inc(dt_done, 1)
                dve.wait_ge(dt_done, b + 1)
                V.tensor_tensor_scan(decay[:, :], in_chunk[:, :], dt_t[:, :], 0.0,
                                     ALU.mult, ALU.add).then_inc(decay_sum, 1)
                dve.wait_ge(decay_sum, b + 1)
                V.tensor_scalar(decay[:, :], decay[:, :], DECAY_MAX, None, ALU.min).then_inc(decay_done, 1)
                dve.wait_ge(decay_done, b + 1)
                if b:
                    dve.wait_ge(alpha_exp, b)
                V.tensor_tensor(dstep[:, 1:N], decay[:, 0:N - 1], decay[:, 1:N], ALU.subtract).then_inc(dstep_done, 1)
                if b:
                    dve.wait_ge(small_exp, b)
                V.tensor_scalar(small[:, 0, :], first_of(decay), -1.0, None, ALU.mult).then_inc(first_done, 1)
                V.tensor_tensor_scan(cumd[:, :], last_of(decay), cum_cap[:, :], 0.0,
                                     ALU.add, ALU.min).then_inc(cumd_done, 1)
                dve.wait_ge(cumd_done, b + 1)
                V.tensor_scalar(ncd[:, :], cumd[:, :], cumd[:, 0:1], DECAY_MAX,
                                ALU.subtract, ALU.min).then_inc(ncd_done, 1)
                dve.wait_ge(ncd_done, b + 1)
                V.tensor_tensor(small[:, 1, 1:NCH], ncd[:, 0:NCH - 1], ncd[:, 1:NCH],
                                ALU.subtract).then_inc(small_done, 1)

            def mixer_cos(b):
                dve.wait_ge(v_up, b + 1)
                if b:
                    dve.wait_ge(v_rot, b)
                V.tensor_tensor(va[:, :], aux_ps[:, :], rope_sb[:, 0, :], ALU.mult).then_inc(v_cos, 1)

            def mixer_sin(b):
                dve.wait_ge(vs_up, b + 1)
                V.tensor_tensor(vb[:, :], aux_ps[:, :], rope_sb[:, 1, :], ALU.mult).then_inc(v_sin, 1)

            def mixer_scan(b):
                dve.wait_ge(alpha_exp, b + 1)
                V.memset(first_of(alpha), 0.0).then_inc(alpha_done, 1)
                dve.wait_ge(alpha_done, b + 1)
                dve.wait_ge(u_ready, b + 1)
                V.tensor_tensor_scan(local[:, :], alpha[:, :], u[:, :], 0.0, ALU.mult, ALU.add).then_inc(local_done, 1)
                dve.wait_ge(local_done, b + 1)
                dve.wait_ge(small_exp, b + 1)
                V.tensor_tensor_scan(carry[:, 1:NCH], last_of(local)[:, 0:NCH - 1], small_e[:, 1, 1:NCH], 0.0,
                                     ALU.add, ALU.mult).then_inc(carry_done, 1)
                dve.wait_ge(carry_done, b + 1)
                V.tensor_tensor(carry_p[:, 1:NCH], carry[:, 1:NCH], small_e[:, 0, 1:NCH],
                                ALU.mult).then_inc(carry_scaled, 1)
                dve.wait_ge(carry_scaled, b + 1)
                V.tensor_tensor(first_of(u)[:, 1:NCH], first_of(u)[:, 1:NCH], carry_p[:, 1:NCH],
                                ALU.add).then_inc(u_seeded, 1)
                dve.wait_ge(u_seeded, b + 1)
                if b:
                    dve.wait_ge(heads_up, b)
                V.tensor_tensor_scan(final[:, :], alpha[:, :], u[:, :], 0.0, ALU.mult, ALU.add).then_inc(final_done, 1)

            def mixer_gated(b):
                dve.wait_ge(gate_tanh, b + 1)
                dve.wait_ge(heads_up, b + 1)
                if b:
                    dve.wait_ge(out_up, b)
                V.scalar_tensor_tensor(gated[:, :], gate_t[:, :], 1.0, aux_ps[:, :],
                                       ALU.add, ALU.mult).then_inc(gated_done, 1)

            def mixer_add(b):
                dve.wait_ge(out_up, b + 1)
                dve.wait_ge(x_plus_h, b + 1)
                xb = xt[:, b, :, :].rearrange("p t d -> p (t d)")
                V.tensor_tensor(xb, aux_ps[:, :], xb, ALU.add).then_inc(x_mixed, 1)

            pass_stats(0)
            pass_normalise(0)
            dve.wait_ge(made_const, 2)
            widen_sum(0)
            route(0)
            coefficients(0)
            dve.wait_ge(proj_in, 16)
            flat = proj_sb[:, :, :].rearrange("p k n -> p (k n)")
            V.tensor_scalar(flat, flat, 0.5, None, ALU.mult).then_inc(made_proj, 1)
            dve.wait_ge(made_ident, 2)
            dve.wait_ge(small_in, 32)
            V.tensor_reduce(head_eye[:, :], ident[:, :].rearrange("p (h d) -> p d h", d=DH), AX_X,
                            ALU.add).then_inc(made_proj, 1)
            dve.wait_ge(made_proj, 2)
            for m in range(H):
                V.tensor_scalar(mix_sb[:, m, :], head_eye[:, :], mix_col[:, m:m + 1], None,
                                ALU.mult).then_inc(made_mix, 1)
            out_bias(0)
            dve.wait_ge(made_const, 8)
            dve.wait_ge(rope_in, 16)
            for slot in range(LAST):
                for q in before_pass(slot, PRE_NORM - 1):
                    pass_stats(q)
                for q in after_pass(slot, POST):
                    update_x(q)
                for b in mixer_at(slot, POST):
                    mixer_stats(b)
                for q in before_pass(slot, PRE_NORM):
                    pass_normalise(q)
                for b in mixer_at(slot, POST + 1):
                    mixer_normalise(b)
                for q in before_pass(slot, PRE_NORM):
                    widen_sum(q)
                for q in before_pass(slot, PRE_ROUTE):
                    route(q)
                    coefficients(q)
                for b in mixer_at(slot, MIX_NORM):
                    mixer_conv(b)
                for b in mixer_at(slot, MIX_DT):
                    mixer_silu(b)
                for q in before_pass(slot, PRE_ROUTE + 2):
                    out_bias(q)
                for b in mixer_at(slot, MIX_DT + 1):
                    mixer_decay(b)
                for b in mixer_at(slot, MIX_V):
                    mixer_cos(b)
                for b in mixer_at(slot, MIX_VS):
                    mixer_sin(b)
                for b in mixer_at(slot, MIX_HEADS - 1):
                    mixer_scan(b)
                for b in mixer_at(slot, MIX_HEADS):
                    mixer_gated(b)
                for b in mixer_at(slot, MIX_OUT):
                    mixer_add(b)


def kernel(L0_attn_x, L0_attn_norm_scale, L0_attn_conv_w, L0_attn_conv_b, L0_attn_in_proj_w, L0_attn_dt_bias,
           L0_attn_head_mix, L0_attn_out_proj_w, L0_ffn_gate_w, L0_ffn_w1, L0_ffn_b1, L0_ffn_w2, L0_ffn_b2):
    import numpy as np
    import concourse.bacc as bacc
    from concourse.bass_utils import run_bass_kernel_spmd

    def arr(a):
        return np.ascontiguousarray(np.asarray(a))

    x = arr(L0_attn_x)
    B, N, D = x.shape
    H = L0_attn_head_mix.shape[0]
    dh = D // H
    E, _, F = L0_ffn_w1.shape
    ft = F // D
    w2 = arr(L0_ffn_w2).reshape(E, ft, D, D).transpose(0, 2, 1, 3).reshape(E, D, F)
    b1 = arr(L0_ffn_b1).reshape(E, ft, D).transpose(0, 2, 1)
    b2 = arr(L0_ffn_b2)[:, :, None]
    wpack = np.concatenate([arr(L0_ffn_w1), w2, b1, b2], axis=2)
    win = arr(L0_attn_in_proj_w)
    swapped = win[:, D:2 * D].reshape(D, H, 2, dh // 2)[:, :, ::-1, :].reshape(D, D)
    proj = np.concatenate([win[:, :2 * D], swapped, win[:, 2 * D:], arr(L0_attn_out_proj_w)], axis=1)
    vecs = np.concatenate([arr(L0_attn_conv_w).reshape(D, -1), arr(L0_attn_conv_b)[:, None],
                           arr(L0_attn_dt_bias)[:, None], arr(L0_attn_norm_scale)[:, None],
                           np.repeat(arr(L0_attn_head_mix), dh, axis=0)], axis=1)
    inv = (1.0 / np.float32(10000.0) ** (np.arange(0, dh, 2, dtype=np.float32) / np.float32(dh))).astype(np.float32)
    ang = (np.arange(N, dtype=np.float32)[None, :] * inv[:, None]).astype(np.float32).astype(np.float64)
    cos, sin = np.cos(ang), np.sin(ang)
    rope = np.stack([np.tile(np.concatenate([cos, cos]), (H, 1)),
                     np.tile(np.concatenate([-sin, sin]), (H, 1))]).astype(np.float32)

    ins = {"x_dram": x, "wpack_dram": wpack, "gate_w_dram": arr(L0_ffn_gate_w), "proj_dram": proj,
           "vecs_dram": vecs, "rope_dram": rope}
    from concourse import mybir as mb
    nc = bacc.Bacc("TRN2", target_bir_lowering=False, num_devices=1)
    aps = []
    for name in list(ins):
        a = ins[name] = np.ascontiguousarray(ins[name])
        aps.append(nc.dram_tensor(name, a.shape, mb.dt.from_np(a.dtype), kind="ExternalInput").ap())
    res = nc.dram_tensor("out_dram", x.shape, mb.dt.float32, kind="ExternalOutput").ap()
    macaron_kernel(nc, *aps, res)
    r = run_bass_kernel_spmd(nc, [ins], core_ids=[0])
    return r.results[0]["out_dram"]
```

```python
from contextlib import ExitStack

import concourse.bass as bass
from concourse import mybir

ALU = mybir.AluOpType
ACT = mybir.ActivationFunctionType
F32 = mybir.dt.float32
F32R = mybir.dt.float32r
U32 = mybir.dt.uint32
AX_X = mybir.AxisListType.X

P = 128
HALF = 512
CHUNK = 32
LN_EPS, RMS_EPS = 1e-5, 1e-6
XN_MAX = 60000.0
DT_MIN, DT_MAX = 0.001, 2.0
DECAY_MAX, CUM_DECAY_MAX = 20.0, 80.0

TICKS = 4
BEFORE = {
    "pe": {"norm": 3, "route": 10},
    "act": {"turn": 3, "tanh": 10, "split_w1": 19},
    "dve": {"stats": 0, "normalise": 3, "widen": 6, "split_z": 4, "route": 8, "coef": 10, "split_w1": 21,
            "bias": 31, "scale_w2": 23},
    "pool": {"rstd": 3},
    "sp": {"load": 8},
}
AFTER = {
    "pe": {"turn_y": 6, "norm": 17, "dt": 30, "v": 32, "vs": 34, "gate": 45, "heads": 52, "out": 57},
    "act": {"out": 3, "scale": 14, "silu": 20, "dt": 31, "decay": 37, "gate": 44, "silu_hi": 26},
    "dve": {"update": 7, "stats": 8, "normalise": 12, "h": 14, "conv": 20, "silu": 22, "cos": 34,
            "sin": 35, "decay": 35, "carry": 37, "u": 40, "scan": 44, "gated": 50, "add": 57,
            "silu_lo": 30},
    "pool": {"rms": 19, "residual": 37},
    "sp": {"store": 8},
}


def macaron_kernel(nc, x, wpack, gate_w, proj, vecs, rope, out):
    B, N, D = x.shape
    E = gate_w.shape[1]
    F = (wpack.shape[2] - 1) // (2 + 1 / P)
    F = int(round(F))
    FT = F // P
    NT = N // P
    NCH = N // CHUNK
    TOP = 2
    SLOTS = TOP * FT
    PASSES = 2 * B
    PACK = wpack.shape[2]
    B1_AT, W2_AT, B2_AT = F, F + FT, 2 * F + FT
    HBUF = 4
    assert D == P and N == 2 * HALF and PACK == 2 * F + FT + 1
    H = vecs.shape[1] - 4 - 3
    DH = D // H

    with ExitStack() as ctx:
        def sb(name, shape, dt=F32):
            return ctx.enter_context(nc.sbuf_tensor(name, shape, dt))

        def sem(name):
            return ctx.enter_context(nc.semaphore(name))

        hid_ps = ctx.enter_context(nc.psum_tensor("hid_ps", [P, 2, N], F32))
        y_ps = ctx.enter_context(nc.psum_tensor("y_ps", [P, N], F32))
        aux_ps = ctx.enter_context(nc.psum_tensor("aux_ps", [P, N], F32))

        xt = sb("xt", [P, B, NT, D])
        ident = sb("ident", [P, P])
        ones = sb("ones", [P, P])
        neg_half = sb("neg_half", [P, 2, NT])
        gate_sb = sb("gate_sb", [P, E])
        proj_sb = sb("proj_sb", [P, 5, P])
        vec_sb = sb("vec_sb", [P, 7 + H])
        conv_w, conv_b = vec_sb[:, 0:4], vec_sb[:, 4:5]
        dt_bias, norm_scale, mix_col = vec_sb[:, 5:6], vec_sb[:, 6:7], vec_sb[:, 7:7 + H]
        rope_sb = sb("rope_sb", [P, 2, N])
        head_eye = sb("head_eye", [P, DH])
        mix_sb = sb("mix_sb", [P, H, DH])
        in_chunk = sb("in_chunk", [P, N])
        cum_cap = sb("cum_cap", [P, NCH])
        w_sb = sb("w_sb", [P, 2, TOP, PACK])
        f_stat = sb("f_stat", [P, NT, 6])
        f_mv = sb("f_mv", [P, NT, 2])
        f_ve = sb("f_ve", [P, NT])
        f_rstd = sb("f_rstd", [P, NT])
        f_tok = sb("f_tok", [P, NT, D])
        z_hi, z_lo = sb("z_hi", [P, 2, N], F32R), sb("z_lo", [P, 2, N], F32R)
        w1_hi, w1_lo = sb("w1_hi", [P, 2, TOP, F], F32R), sb("w1_lo", [P, 2, TOP, F], F32R)
        zsum = sb("zsum", [P, 1])
        zsum_wide = sb("zsum_wide", [P, P])
        logit = sb("logit", [P, E])
        top_v = sb("top_v", [P, 8])
        top_i = sb("top_i", [P, 8], U32)
        top_d = sb("top_d", [P, 1])
        top_t = sb("top_t", [P, 1])
        coef = sb("coef", [P, 2, TOP])
        bias2a = sb("bias2a", [P, 1])
        bias2 = sb("bias2", [P, 2, 1])
        hid = sb("hid", [P, HBUF, N])
        yt = sb("yt", [P, N])
        m_stat = sb("m_stat", [P, NT, 6])
        m_mv = sb("m_mv", [P, NT, 2])
        m_var = sb("m_var", [P, 2, NT])
        m_inv = sb("m_inv", [P, 2, NT])
        m_h = sb("m_h", [P, NT, D])
        m_tok = sb("m_tok", [P, NT, D])
        PAD = 3
        xs = sb("xs", [P, PAD + N])
        xc = sb("xc", [P, N])
        xc_tanh = sb("xc_tanh", [P, N])
        silu = sb("silu", [P, N])
        silu_hi, silu_lo = sb("silu_hi", [P, N], F32R), sb("silu_lo", [P, N], F32R)
        proj_hi, proj_lo = sb("proj_hi", [P, 4, P], F32R), sb("proj_lo", [P, 4, P], F32R)
        dt_e = sb("dt_e", [P, N])
        dt_raw = sb("dt_raw", [P, N])
        dt_t = sb("dt_t", [P, N])
        decay = sb("decay", [P, N])
        dstep = sb("dstep", [P, N])
        alpha = sb("alpha", [P, N])
        small = sb("small", [P, 2, NCH])
        small_e = sb("small_e", [P, 2, NCH])
        cumd = sb("cumd", [P, NCH])
        ncd = sb("ncd", [P, NCH])
        carry = sb("carry", [P, NCH])
        carry_p = sb("carry_p", [P, NCH])
        va = sb("va", [P, N])
        vb = sb("vb", [P, N])
        vr = sb("vr", [P, N])
        u = sb("u", [P, N])
        local = sb("local", [P, N])
        final = sb("final", [P, N])
        gate_t = sb("gate_t", [P, N])
        gated = sb("gated", [P, N])

        def first_of(t):
            return t[:, :].rearrange("p (c t) -> p c t", t=CHUNK)[:, :, 0]

        def last_of(t):
            return t[:, :].rearrange("p (c t) -> p c t", t=CHUNK)[:, :, CHUNK - 1]

        x_in = [sem(f"x_in{b}") for b in range(B)]
        x_in_tail = sem("x_in_tail")
        proj_in, rope_in, small_in, vecs_in = sem("proj_in"), sem("rope_in"), sem("small_in"), sem("vecs_in")
        w1_in = [[sem(f"w1_in{i}_{k}") for k in range(TOP)] for i in range(2)]
        w2_in = [sem(f"w2_in{i}") for i in range(2)]
        out_done = sem("out_done")
        made_ident, made_const, made_proj, made_mix = (
            sem("made_ident"), sem("made_const"), sem("made_proj"), sem("made_mix"))
        f_stats_step, f_aggr_done = sem("f_stats_step"), sem("f_aggr_done")
        f_var_eps, f_rstd_done, f_norm_done = sem("f_var_eps"), sem("f_rstd_done"), sem("f_norm_done")
        f_rstd_head, zwide_up = sem("f_rstd_head"), sem("zwide_up")
        f_turned, zt_ready, zwide_ready = sem("f_turned"), sem("zt_ready"), sem("zwide_ready")
        logits_up, logits_read, top_ready = sem("logits_up"), sem("logits_read"), sem("top_ready")
        index_ready, diff_ready, tanh_ready, coef_ready = (
            sem("index_ready"), sem("diff_ready"), sem("tanh_ready"), sem("coef_ready"))
        zlo_ready, w1_hi_ready, w1_lo_ready = sem("zlo_ready"), sem("w1_hi_ready"), sem("w1_lo_ready")
        bias2a_ready, bias2_ready, w2_scaled = sem("bias2a_ready"), sem("bias2_ready"), sem("w2_scaled")
        hid_up, hid_ready, hid_used = sem("hid_up"), sem("hid_ready"), sem("hid_used")
        yt_ready, y_turned, x_updated = sem("yt_ready"), sem("y_turned"), sem("x_updated")
        m_stats_step, m_aggr_done, m_pool_step = sem("m_stats_step"), sem("m_aggr_done"), sem("m_pool_step")
        m_h_done, m_norm_done, x_plus_h = sem("m_h_done"), sem("m_norm_done"), sem("x_plus_h")
        m_turned, xs_ready, xs_clipped, conv_step = (
            sem("m_turned"), sem("xs_ready"), sem("xs_clipped"), sem("conv_step"))
        silu_tanh, silu_done = sem("silu_tanh"), sem("silu_done")
        silu_hi_done, silu_lo_done, proj_hi_ready = sem("silu_hi_done"), sem("silu_lo_done"), sem("proj_hi_ready")
        dt_up, dt_exp, dt_ln, dt_done = sem("dt_up"), sem("dt_exp"), sem("dt_ln"), sem("dt_done")
        decay_sum, decay_done, dstep_done, first_done = (
            sem("decay_sum"), sem("decay_done"), sem("dstep_done"), sem("first_done"))
        cumd_done, ncd_done, small_done = sem("cumd_done"), sem("ncd_done"), sem("small_done")
        alpha_exp, small_exp, alpha_done = sem("alpha_exp"), sem("small_exp"), sem("alpha_done")
        v_up, v_cos, vs_up, v_sin, v_rot, u_ready = (
            sem("v_up"), sem("v_cos"), sem("vs_up"), sem("v_sin"), sem("v_rot"), sem("u_ready"))
        local_done, carry_done, carry_scaled, u_seeded, final_done = (
            sem("local_done"), sem("carry_done"), sem("carry_scaled"), sem("u_seeded"), sem("final_done"))
        gate_up, gate_tanh, heads_up, gated_done, out_up, x_mixed = (
            sem("gate_up"), sem("gate_tanh"), sem("heads_up"), sem("gated_done"), sem("out_up"), sem("x_mixed"))

        PERIOD = TICKS * SLOTS
        LAST = PASSES * PERIOD + max(AFTER[e][k] for e, k in (("pe", "turn_y"), ("dve", "update"), ("sp", "store"))) + 1

        def after_pass(tick, offset):
            q, r = divmod(tick - offset, PERIOD)
            return [q - 1] if r == 0 and 1 <= q <= PASSES else []

        def mixer_at(tick, offset):
            return [b for b in after_pass(tick, offset) if b < B]

        def before_pass(tick, offset, first=1):
            q, r = divmod(tick - offset, PERIOD)
            return [q + 1] if r == 0 and first <= q + 1 < PASSES else []

        def parts_of(q, n):
            return [slice(0, n)] if q < PASSES - 1 else [slice(0, n // 2), slice(n // 2, n)]

        def up_at(tick):
            return [tick // TICKS] if tick % TICKS == 0 and tick // TICKS < PASSES * SLOTS else []

        def down_at(tick):
            return [tick // TICKS - 1] if tick % TICKS == TICKS // 2 and 1 <= tick // TICKS <= PASSES * SLOTS else []

        block = ctx.enter_context(nc.Block())

        @block.sync
        def _(sp):
            def load_x(b):
                sp.dma_start(xt[:, b, :, :], x[b].rearrange("(t p) d -> p t d", p=P)).then_inc(x_in[b], 16)

            def load_experts(q):
                if q >= 2:
                    sp.wait_ge(hid_used, SLOTS * (q - 1))
                    sp.wait_ge(bias2_ready, q - 1)
                sp.wait_ge(index_ready, q + 1)
                src = []
                for k in range(TOP):
                    e = sp.value_load(top_i[0:1, k:k + 1], min_val=0, max_val=E - 1)
                    src.append(wpack[bass.ds(e, 1), :, :].rearrange("e p n -> p (e n)"))
                    sp.dma_start(w_sb[:, q % 2, k, 0:W2_AT], src[k][:, 0:W2_AT]).then_inc(w1_in[q % 2][k], 16)
                for k in range(TOP):
                    sp.dma_start(w_sb[:, q % 2, k, W2_AT:], src[k][:, W2_AT:]).then_inc(w2_in[q % 2], 16)

            x0 = x[0].rearrange("(t p) d -> p t d", p=P)
            sp.dma_start(xt[:, 0, 0:NT // 2, :], x0[:, 0:NT // 2, :]).then_inc(x_in[0], 16)
            sp.dma_start(gate_sb[:, :], gate_w).then_inc(small_in, 16)
            load_x(1)
            load_experts(0)
            load_x(2)
            load_x(3)
            for tick in range(LAST):
                for q in after_pass(tick, AFTER["sp"]["store"]):
                    if q >= B:
                        for i, tiles in enumerate(parts_of(q, NT)):
                            sp.wait_ge(x_updated, q + 1 + i)
                            sp.dma_start(out[q - B].rearrange("(t p) d -> p t d", p=P)[:, tiles, :],
                                         xt[:, q - B, tiles, :]).then_inc(out_done, 16)
                for q in before_pass(tick, BEFORE["sp"]["load"]):
                    load_experts(q)
            sp.wait_ge(out_done, 16 * (B + 1))

        @block.gpsimd
        def _(pool):
            nc.gpsimd.memset(ident[:, :], 0.0).then_inc(made_ident, 1)
            pool.wait_ge(made_ident, 1)
            nc.gpsimd.affine_select(out=ident[:, :], in_=ident[:, :], compare_op=ALU.not_equal, fill=1.0,
                                    base=0, pattern=[[-1, P]], channel_multiplier=1).then_inc(made_ident, 1)
            nc.gpsimd.memset(neg_half[:, :, :], -0.5).then_inc(made_const, 1)
            nc.gpsimd.memset(ones[:, :], 1.0).then_inc(made_const, 1)
            nc.gpsimd.memset(xs[:, 0:PAD], 0.0).then_inc(made_const, 1)
            nc.gpsimd.memset(dstep[:, 0:1], 0.0).then_inc(made_const, 1)
            nc.gpsimd.memset(small[:, 1, 0:1], 0.0).then_inc(made_const, 1)
            nc.gpsimd.memset(cum_cap[:, :], CUM_DECAY_MAX).then_inc(made_const, 1)
            pool.dma_start(proj_sb[:, :, :], proj.rearrange("p (k n) -> p k n", n=P)).then_inc(proj_in, 16)
            pool.dma_start(rope_sb[:, :, :], rope.rearrange("k p n -> p k n")).then_inc(rope_in, 16)

            def rstd_of(q, tiles, step, done):
                nc.gpsimd.tensor_scalar(f_ve[:, tiles], f_mv[:, tiles, 1], LN_EPS, None, ALU.add).then_inc(f_var_eps, 1)
                pool.wait_ge(f_var_eps, step)
                nc.gpsimd.tensor_tensor(f_rstd[:, tiles], f_ve[:, tiles], neg_half[:, 0, tiles],
                                        ALU.pow).then_inc(done, 1)

            def pass_rstd(q):
                if q == 0:
                    pool.wait_ge(f_aggr_done, NT // 2)
                    rstd_of(q, slice(0, NT // 2), 1, f_rstd_head)
                    pool.wait_ge(f_aggr_done, NT)
                    rstd_of(q, slice(NT // 2, NT), 2, f_rstd_done)
                else:
                    pool.wait_ge(f_aggr_done, NT * (q + 1))
                    pool.wait_ge(f_norm_done, NT * q)
                    rstd_of(q, slice(0, NT), q + 2, f_rstd_done)

            def mixer_rms(b):
                pool.wait_ge(m_aggr_done, NT * (b + 1))
                if b:
                    pool.wait_ge(m_h_done, NT * b)
                nc.gpsimd.tensor_scalar(m_var[:, 0, :], m_mv[:, :, 1], LN_EPS, None, ALU.add).then_inc(m_pool_step, 1)
                nc.gpsimd.tensor_scalar(m_var[:, 1, :], m_mv[:, :, 1], 1.0 + RMS_EPS, LN_EPS * RMS_EPS,
                                        ALU.mult, ALU.add).then_inc(m_pool_step, 1)
                pool.wait_ge(m_pool_step, 3 * b + 2)
                nc.gpsimd.tensor_tensor(m_inv[:, :, :], m_var[:, :, :], neg_half[:, :, :],
                                        ALU.pow).then_inc(m_pool_step, 1)

            def mixer_residual(b):
                pool.wait_ge(m_h_done, NT * (b + 1))
                xb = xt[:, b, :, :]
                nc.gpsimd.tensor_tensor(xb, xb, m_h[:, :, :], ALU.add).then_inc(x_plus_h, 1)

            pool.wait_ge(made_const, 2)
            pass_rstd(0)
            nc.gpsimd.memset(in_chunk[:, :], 1.0).then_inc(made_const, 1)
            pool.wait_ge(made_const, 7)
            nc.gpsimd.memset(first_of(in_chunk), 0.0).then_inc(made_const, 1)
            pass_rstd(1)
            before, after = BEFORE["pool"], AFTER["pool"]
            for tick in range(LAST):
                for q in before_pass(tick, before["rstd"], 2):
                    pass_rstd(q)
                for b in mixer_at(tick, after["rms"]):
                    mixer_rms(b)
                for b in mixer_at(tick, after["residual"]):
                    mixer_residual(b)

        @block.scalar
        def _(act):
            def turn_z(q):
                act.wait_ge(f_turned, q + 1)
                if q >= 2:
                    act.wait_ge(hid_up, SLOTS * (q - 1))
                if q:
                    act.wait_ge(zwide_ready, q)
                nc.scalar.activation(z_hi[:, q % 2, :], aux_ps[:, :], ACT.Copy,
                                     accum_out=zsum[:, :]).then_inc(zt_ready, 1)

            def top_tanh(q):
                act.wait_ge(diff_ready, q + 1)
                nc.scalar.activation(top_t[:, :], top_d[:, :], ACT.Tanh, scale=0.5 / N).then_inc(tanh_ready, 1)

            def split_w1(q):
                if q >= 2:
                    act.wait_ge(hid_up, SLOTS * (q - 1))
                for k in range(TOP):
                    act.wait_ge(w1_in[q % 2][k], 16 * (q // 2 + 1))
                    nc.scalar.activation(w1_hi[:, q % 2, k, :], w_sb[:, q % 2, k, 0:F],
                                         ACT.Copy).then_inc(w1_hi_ready, 1)

            def gelu(slot):
                q, t = divmod(slot, SLOTS)
                act.wait_ge(hid_up, slot + 1)
                if slot >= HBUF:
                    act.wait_ge(hid_used, slot - HBUF + 1)
                k, f = divmod(t, FT)
                bias = w_sb[:, q % 2, k, B1_AT + f:B1_AT + f + 1]
                nc.scalar.activation(hid[:, slot % HBUF, :], hid_ps[:, slot % 2, :], ACT.Gelu,
                                     bias=bias).then_inc(hid_ready, 1)

            def pass_out(q):
                act.wait_ge(bias2_ready, q + 1)
                if q:
                    act.wait_ge(y_turned, q)
                for i, cols in enumerate(parts_of(q, N)):
                    act.wait_ge(hid_used, SLOTS * (q + 1) + i)
                    nc.scalar.activation(yt[:, cols], y_ps[:, cols], ACT.Identity,
                                         bias=bias2[:, q % 2, :]).then_inc(yt_ready, 1)

            def mixer_scale(b):
                act.wait_ge(m_turned, b + 1)
                if b:
                    act.wait_ge(conv_step, 4 * b)
                nc.scalar.activation(xs[:, PAD:], aux_ps[:, :], ACT.Copy, scale=norm_scale).then_inc(xs_ready, 1)

            def mixer_silu(b):
                act.wait_ge(conv_step, 4 * (b + 1))
                if b:
                    act.wait_ge(silu_done, b)
                nc.scalar.activation(xc_tanh[:, :], xc[:, :], ACT.Tanh, scale=0.5).then_inc(silu_tanh, 1)

            def mixer_silu_hi(b):
                act.wait_ge(silu_done, b + 1)
                if b:
                    act.wait_ge(gate_up, b)
                nc.scalar.activation(silu_hi[:, :], silu[:, :], ACT.Copy).then_inc(silu_hi_done, 1)

            def mixer_dt(b):
                nc.scalar.preload_act_table_set("natural_log_exp_and_others")
                act.wait_ge(dt_up, b + 1)
                if b:
                    act.wait_ge(dt_done, b)
                nc.scalar.activation(dt_e[:, :], aux_ps[:, :], ACT.Exp, bias=dt_bias).then_inc(dt_exp, 1)
                act.wait_ge(dt_exp, b + 1)
                nc.scalar.activation(dt_raw[:, :], dt_e[:, :], ACT.Ln, bias=1.0).then_inc(dt_ln, 1)
                nc.scalar.preload_act_table_set("gelu_and_others")

            def mixer_decay(b):
                nc.scalar.preload_act_table_set("natural_log_exp_and_others")
                act.wait_ge(dstep_done, b + 1)
                if b:
                    act.wait_ge(final_done, b)
                nc.scalar.activation(alpha[:, :], dstep[:, :], ACT.Exp).then_inc(alpha_exp, 1)
                act.wait_ge(small_done, b + 1)
                nc.scalar.activation(small_e[:, :, :], small[:, :, :], ACT.Exp).then_inc(small_exp, 1)
                nc.scalar.preload_act_table_set("gelu_and_others")

            def mixer_gate(b):
                act.wait_ge(gate_up, b + 1)
                if b:
                    act.wait_ge(gated_done, b)
                nc.scalar.activation(gate_t[:, :], aux_ps[:, :], ACT.Tanh, scale=0.5).then_inc(gate_tanh, 1)

            x0 = x[0].rearrange("(t p) d -> p t d", p=P)
            act.dma_start(xt[:, 0, NT // 2:, :], x0[:, NT // 2:, :]).then_inc(x_in_tail, 16)
            act.dma_start(vec_sb[:, :], vecs).then_inc(vecs_in, 16)
            nc.scalar.preload_act_table_set("gelu_and_others")
            turn_z(0)
            top_tanh(0)
            split_w1(0)
            act.wait_ge(made_proj, 1)
            nc.scalar.activation(proj_hi[:, :, :], proj_sb[:, 0:4, :], ACT.Copy).then_inc(proj_hi_ready, 1)
            act.wait_ge(vecs_in, 16)
            act.wait_ge(made_const, 6)
            before, after = BEFORE["act"], AFTER["act"]
            for tick in range(LAST):
                for slot in up_at(tick):
                    gelu(slot)
                for b in mixer_at(tick, after["silu"]):
                    mixer_silu(b)
                for q in after_pass(tick, after["out"]):
                    pass_out(q)
                for q in before_pass(tick, before["turn"]):
                    turn_z(q)
                for q in before_pass(tick, before["tanh"]):
                    top_tanh(q)
                for q in before_pass(tick, before["split_w1"]):
                    split_w1(q)
                for b in mixer_at(tick, after["scale"]):
                    mixer_scale(b)
                for b in mixer_at(tick, after["silu_hi"]):
                    mixer_silu_hi(b)
                for b in mixer_at(tick, after["dt"]):
                    mixer_dt(b)
                for b in mixer_at(tick, after["decay"]):
                    mixer_decay(b)
                for b in mixer_at(tick, after["gate"]):
                    mixer_gate(b)

        @block.tensor
        def _(pe):
            def up(slot):
                q, t = divmod(slot, SLOTS)
                k, f = divmod(t, FT)
                if f == 0:
                    pe.wait_ge(w1_hi_ready, TOP * q + k + 1)
                if t == 0:
                    pe.wait_ge(zt_ready, q + 1)
                    pe.wait_ge(zlo_ready, q + 1)
                if slot >= 2:
                    pe.wait_ge(hid_ready, slot - 1)
                rows = slice(f * P, (f + 1) * P)
                hi, lo = w1_hi[:, q % 2, k, rows], w1_lo[:, q % 2, k, rows]
                for w, z, first, end in ((hi, z_hi, True, False), (hi, z_lo, False, False), (lo, z_hi, False, True)):
                    if f == 0 and w is lo:
                        pe.wait_ge(w1_lo_ready, TOP * q + k + 1)
                    for h in range(2):
                        cols = slice(h * HALF, (h + 1) * HALF)
                        last = nc.tensor.matmul(hid_ps[:, slot % 2, cols], w, z[:, q % 2, cols],
                                                start=first, stop=end)
                last.then_inc(hid_up, 1)

            def down(slot):
                q, t = divmod(slot, SLOTS)
                k, f = divmod(t, FT)
                pe.wait_ge(hid_ready, slot + 1)
                if f == 0:
                    pe.wait_ge(w2_scaled, TOP * q + k + 1)
                if t == 0 and q:
                    pe.wait_ge(yt_ready, q)
                w2 = w_sb[:, q % 2, k, W2_AT + f * P:W2_AT + (f + 1) * P]
                for h in range(2):
                    cols = slice(h * HALF, (h + 1) * HALF)
                    last = nc.tensor.matmul(y_ps[:, cols], w2, hid[:, slot % HBUF, cols],
                                            start=t == 0, stop=t == SLOTS - 1)
                    if slot == PASSES * SLOTS - 1 and h == 0:
                        last.then_inc(hid_used, 1)
                last.then_inc(hid_used, 1)

            reader = []

            def take_aux(*next_reader):
                if reader:
                    pe.wait_ge(*reader.pop())
                reader.append(next_reader)

            def turn(tiles, tile_ready, before):
                for t in range(NT):
                    pe.wait_ge(tile_ready, before + t + 1)
                    last = nc.tensor.transpose(aux_ps[:, t * P:(t + 1) * P], tiles(t), ident[:, :])
                return last

            def pre_norm(q):
                take_aux(zlo_ready, q + 1)
                turn(lambda t: f_tok[:, t, :], f_norm_done, NT * q).then_inc(f_turned, 1)

            def pre_route(q):
                pe.wait_ge(zwide_ready, q + 1)
                take_aux(logits_read, q + 1)
                nc.tensor.matmul(aux_ps[:, 0:E], zsum_wide[:, :], gate_sb[:, :],
                                 start=True, stop=True).then_inc(logits_up, 1)

            def post(q):
                take_aux(x_updated, q + 1)
                for i, tiles in enumerate(parts_of(q, NT)):
                    pe.wait_ge(yt_ready, q + 1 + i)
                    for t in range(NT)[tiles]:
                        cols = slice(t * P, (t + 1) * P)
                        last = nc.tensor.transpose(aux_ps[:, cols], yt[:, cols], ident[:, :])
                    last.then_inc(y_turned, 1)

            def mixer_norm(b):
                take_aux(xs_ready, b + 1)
                turn(lambda t: m_tok[:, t, :], m_norm_done, NT * b).then_inc(m_turned, 1)

            def project_silu(b, w, done):
                if w == 0:
                    pe.wait_ge(silu_hi_done, b + 1)
                    if b == 0:
                        pe.wait_ge(made_proj, 3)
                for wt, z, first, end in ((proj_hi, silu_hi, True, False), (proj_lo, silu_hi, False, False),
                                          (proj_hi, silu_lo, False, True)):
                    if w == 0 and z is silu_lo:
                        pe.wait_ge(silu_lo_done, b + 1)
                    for h in range(2):
                        cols = slice(h * HALF, (h + 1) * HALF)
                        last = nc.tensor.matmul(aux_ps[:, cols], wt[:, w, :], z[:, cols], start=first, stop=end)
                last.then_inc(done, 1)

            def mixer_dt(b):
                take_aux(dt_exp, b + 1)
                project_silu(b, 0, dt_up)

            def mixer_v(b):
                take_aux(v_cos, b + 1)
                project_silu(b, 1, v_up)

            def mixer_vs(b):
                take_aux(v_sin, b + 1)
                project_silu(b, 2, vs_up)

            def mixer_gate(b):
                take_aux(gate_tanh, b + 1)
                project_silu(b, 3, gate_up)

            def mixer_heads(b):
                pe.wait_ge(final_done, b + 1)
                if b == 0:
                    pe.wait_ge(made_mix, 1)
                take_aux(gated_done, b + 1)
                for h in range(2):
                    cols = slice(h * HALF, (h + 1) * HALF)
                    last = nc.tensor.matmul(aux_ps[:, cols], mix_sb[:, :, :].rearrange("p m d -> p (m d)"),
                                            final[:, cols], start=True, stop=True)
                last.then_inc(heads_up, 1)

            def mixer_out(b):
                pe.wait_ge(gated_done, b + 1)
                take_aux(x_mixed, b + 1)
                for t in range(NT):
                    cols = slice(t * P, (t + 1) * P)
                    last = nc.tensor.matmul(aux_ps[:, cols], gated[:, cols], proj_sb[:, 4, :],
                                            start=True, stop=True)
                last.then_inc(out_up, 1)

            pe.wait_ge(made_const, 2)
            for t in range(NT):
                pe.wait_ge(f_norm_done, t + 1)
                last = nc.tensor.matmul(y_ps[:, 0:P], f_tok[:, t, :], ones[:, :], start=t == 0, stop=t == NT - 1)
            last.then_inc(zwide_up, 1)
            pe.wait_ge(small_in, 16)
            pe.wait_ge(zwide_ready, 1)
            nc.tensor.matmul(y_ps[:, HALF:HALF + E], zsum_wide[:, :], gate_sb[:, :],
                             start=True, stop=True).then_inc(logits_up, 1)
            pe.wait_ge(made_ident, 2)
            pre_norm(0)
            before, after = BEFORE["pe"], AFTER["pe"]
            for tick in range(LAST):
                for slot in up_at(tick):
                    up(slot)
                for slot in down_at(tick):
                    down(slot)
                for q in after_pass(tick, after["turn_y"]):
                    post(q)
                for q in before_pass(tick, before["norm"]):
                    pre_norm(q)
                for q in before_pass(tick, before["route"]):
                    pre_route(q)
                for b in mixer_at(tick, after["norm"]):
                    mixer_norm(b)
                for b in mixer_at(tick, after["dt"]):
                    mixer_dt(b)
                for b in mixer_at(tick, after["v"]):
                    mixer_v(b)
                for b in mixer_at(tick, after["vs"]):
                    mixer_vs(b)
                for b in mixer_at(tick, after["gate"]):
                    mixer_gate(b)
                for b in mixer_at(tick, after["heads"]):
                    mixer_heads(b)
                for b in mixer_at(tick, after["out"]):
                    mixer_out(b)

        @block.vector
        def _(dve):
            V = nc.vector

            def pass_stats(q):
                b = q % B
                if q < B:
                    dve.wait_ge(x_in[b], 16)
                else:
                    dve.wait_ge(x_mixed, b + 1)
                if q:
                    dve.wait_ge(f_rstd_done, q)
                for tiles in (range(0, NT // 2), range(NT // 2, NT)) if q == 0 else (range(NT),):
                    if q == 0 and tiles[0]:
                        dve.wait_ge(x_in_tail, 16)
                    for t in tiles:
                        V.bn_stats(f_stat[:, t, :], xt[:, b, t, :]).then_inc(f_stats_step, 1)
                    for t in tiles:
                        dve.wait_ge(f_stats_step, NT * q + t + 1)
                        V.bn_aggr(f_mv[:, t, :], f_stat[:, t, :]).then_inc(f_aggr_done, 1)

            def pass_normalise(q):
                if q:
                    dve.wait_ge(f_rstd_done, q + 1)
                    dve.wait_ge(f_turned, q)
                dve.wait_ge(f_aggr_done, NT * (q + 1))
                for t in range(NT):
                    if q == 0 and t == 0:
                        dve.wait_ge(f_rstd_head, 1)
                    if q == 0 and t == NT // 2:
                        dve.wait_ge(f_rstd_done, 1)
                    V.tensor_scalar(f_tok[:, t, :], xt[:, q % B, t, :], f_mv[:, t, 0:1], f_rstd[:, t:t + 1],
                                    ALU.subtract, ALU.mult).then_inc(f_norm_done, 1)

            def split_z(q):
                dve.wait_ge(zt_ready, q + 1)
                if q >= 2:
                    dve.wait_ge(hid_up, SLOTS * (q - 1))
                V.tensor_tensor(z_lo[:, q % 2, :], aux_ps[:, :], z_hi[:, q % 2, :].bitcast(F32),
                                ALU.subtract).then_inc(zlo_ready, 1)

            def split_w1(q):
                if q >= 2:
                    dve.wait_ge(hid_up, SLOTS * (q - 1))
                for k in range(TOP):
                    dve.wait_ge(w1_hi_ready, TOP * q + k + 1)
                    V.tensor_tensor(w1_lo[:, q % 2, k, :], w_sb[:, q % 2, k, 0:F],
                                    w1_hi[:, q % 2, k, :].bitcast(F32), ALU.subtract).then_inc(w1_lo_ready, 1)

            def widen_sum(q):
                dve.wait_ge(zt_ready, q + 1)
                if q:
                    dve.wait_ge(logits_up, q)
                V.tensor_scalar(zsum_wide[:, :], ones[:, :], zsum[:, 0:1], None, ALU.mult).then_inc(zwide_ready, 1)

            def route(q):
                dve.wait_ge(logits_up, q + 1)
                logits = aux_ps[:, 0:E] if q else y_ps[:, HALF:HALF + E]
                V.tensor_copy(logit[:, :], logits).then_inc(logits_read, 1)
                dve.wait_ge(logits_read, q + 1)
                V.max(top_v[:, :], logit[:, :]).then_inc(top_ready, 1)
                dve.wait_ge(top_ready, q + 1)
                if q:
                    dve.wait_ge(w2_in[(q - 1) % 2], 16 * TOP * ((q - 1) // 2 + 1))
                V.max_index(top_i[:, :], top_v[:, :], logit[:, :]).then_inc(index_ready, 1)
                if q:
                    dve.wait_ge(tanh_ready, q)
                V.tensor_tensor(top_d[:, :], top_v[:, 0:1], top_v[:, 1:2], ALU.subtract).then_inc(diff_ready, 1)

            def coefficients(q):
                dve.wait_ge(tanh_ready, q + 1)
                for k in range(TOP):
                    V.tensor_scalar(coef[:, q % 2, k:k + 1], top_t[:, :], 0.25 if k == 0 else -0.25, 0.25,
                                    ALU.mult, ALU.add).then_inc(coef_ready, 1)

            def scale_w2(q):
                dve.wait_ge(w2_in[q % 2], 16 * TOP * (q // 2 + 1))
                dve.wait_ge(coef_ready, TOP * (q + 1))
                for k in range(TOP):
                    w2 = w_sb[:, q % 2, k, W2_AT:W2_AT + F]
                    V.tensor_scalar(w2, w2, coef[:, q % 2, k:k + 1], None, ALU.mult).then_inc(w2_scaled, 1)

            def out_bias(q):
                dve.wait_ge(w2_in[q % 2], 16 * TOP * (q // 2 + 1))
                dve.wait_ge(coef_ready, TOP * (q + 1))
                b2 = [w_sb[:, q % 2, k, B2_AT:B2_AT + 1] for k in range(TOP)]
                V.tensor_scalar(bias2a[:, :], b2[0], coef[:, q % 2, 0:1], None, ALU.mult).then_inc(bias2a_ready, 1)
                dve.wait_ge(bias2a_ready, q + 1)
                V.scalar_tensor_tensor(bias2[:, q % 2, :], b2[1], coef[:, q % 2, 1:2], bias2a[:, :],
                                       ALU.mult, ALU.add).then_inc(bias2_ready, 1)

            def update_x(q):
                xb = xt[:, q % B, :, :].rearrange("p t d -> p (t d)")
                for i, cols in enumerate(parts_of(q, N)):
                    dve.wait_ge(y_turned, q + 1 + i)
                    V.tensor_tensor(xb[:, cols], aux_ps[:, cols], xb[:, cols], ALU.add).then_inc(x_updated, 1)

            def mixer_stats(b):
                dve.wait_ge(x_updated, b + 1)
                for t in range(NT):
                    V.bn_stats(m_stat[:, t, :], xt[:, b, t, :]).then_inc(m_stats_step, 1)
                if b:
                    dve.wait_ge(m_pool_step, 3 * b)
                    dve.wait_ge(m_h_done, NT * b)
                for t in range(NT):
                    dve.wait_ge(m_stats_step, NT * b + t + 1)
                    V.bn_aggr(m_mv[:, t, :], m_stat[:, t, :]).then_inc(m_aggr_done, 1)

            def mixer_normalise(b):
                dve.wait_ge(m_pool_step, 3 * (b + 1))
                dve.wait_ge(m_aggr_done, NT * (b + 1))
                if b:
                    dve.wait_ge(m_turned, b)
                for t in range(NT):
                    V.tensor_scalar(m_tok[:, t, :], xt[:, b, t, :], m_mv[:, t, 0:1], m_inv[:, 1, t:t + 1],
                                    ALU.subtract, ALU.mult).then_inc(m_norm_done, 1)
            def mixer_h(b):
                dve.wait_ge(m_pool_step, 3 * (b + 1))
                if b:
                    dve.wait_ge(x_plus_h, b)
                for t in range(NT):
                    V.tensor_scalar(m_h[:, t, :], xt[:, b, t, :], m_mv[:, t, 0:1], m_inv[:, 0, t:t + 1],
                                    ALU.subtract, ALU.mult).then_inc(m_h_done, 1)

            def mixer_conv(b):
                dve.wait_ge(xs_ready, b + 1)
                V.tensor_scalar(xs[:, PAD:], xs[:, PAD:], XN_MAX, -XN_MAX, ALU.min, ALU.max).then_inc(xs_clipped, 1)
                dve.wait_ge(xs_clipped, b + 1)
                V.tensor_scalar(xc[:, :], xs[:, 0:N], conv_w[:, 0:1], conv_b, ALU.mult, ALU.add).then_inc(conv_step, 1)
                for k in range(1, 4):
                    dve.wait_ge(conv_step, 4 * b + k)
                    V.scalar_tensor_tensor(xc[:, :], xs[:, k:k + N], conv_w[:, k:k + 1], xc[:, :],
                                           ALU.mult, ALU.add).then_inc(conv_step, 1)

            def mixer_silu(b):
                dve.wait_ge(silu_tanh, b + 1)
                if b:
                    dve.wait_ge(silu_lo_done, b)
                V.scalar_tensor_tensor(silu[:, :], xc_tanh[:, :], 1.0, xc[:, :],
                                       ALU.add, ALU.mult).then_inc(silu_done, 1)

            def mixer_silu_lo(b):
                dve.wait_ge(silu_hi_done, b + 1)
                if b:
                    dve.wait_ge(gate_up, b)
                V.tensor_tensor(silu_lo[:, :], silu[:, :], silu_hi[:, :].bitcast(F32),
                                ALU.subtract).then_inc(silu_lo_done, 1)

            def mixer_decay(b):
                dve.wait_ge(dt_ln, b + 1)
                V.tensor_scalar(dt_t[:, :], dt_raw[:, :], DT_MIN, DT_MAX, ALU.max, ALU.min).then_inc(dt_done, 1)
                dve.wait_ge(dt_done, b + 1)
                V.tensor_tensor_scan(decay[:, :], in_chunk[:, :], dt_t[:, :], 0.0,
                                     ALU.mult, ALU.add).then_inc(decay_sum, 1)
                dve.wait_ge(decay_sum, b + 1)
                V.tensor_scalar(decay[:, :], decay[:, :], DECAY_MAX, None, ALU.min).then_inc(decay_done, 1)
                dve.wait_ge(decay_done, b + 1)
                if b:
                    dve.wait_ge(alpha_exp, b)
                V.tensor_tensor(dstep[:, 1:N], decay[:, 0:N - 1], decay[:, 1:N], ALU.subtract).then_inc(dstep_done, 1)

            def mixer_carry_decay(b):
                dve.wait_ge(decay_done, b + 1)
                if b:
                    dve.wait_ge(small_exp, b)
                V.tensor_scalar(small[:, 0, :], first_of(decay), -1.0, None, ALU.mult).then_inc(first_done, 1)
                V.tensor_tensor_scan(cumd[:, :], last_of(decay), cum_cap[:, :], 0.0,
                                     ALU.add, ALU.min).then_inc(cumd_done, 1)
                dve.wait_ge(cumd_done, b + 1)
                V.tensor_scalar(ncd[:, :], cumd[:, :], cumd[:, 0:1], DECAY_MAX,
                                ALU.subtract, ALU.min).then_inc(ncd_done, 1)
                dve.wait_ge(ncd_done, b + 1)
                V.tensor_tensor(small[:, 1, 1:NCH], ncd[:, 0:NCH - 1], ncd[:, 1:NCH],
                                ALU.subtract).then_inc(small_done, 1)

            def mixer_input(b):
                dve.wait_ge(v_sin, b + 1)
                V.tensor_tensor(vr[:, :], va[:, :], vb[:, :], ALU.add).then_inc(v_rot, 1)
                dve.wait_ge(v_rot, b + 1)
                V.tensor_tensor(u[:, :], vr[:, :], dt_t[:, :], ALU.mult).then_inc(u_ready, 1)

            def mixer_cos(b):
                dve.wait_ge(v_up, b + 1)
                V.tensor_tensor(va[:, :], aux_ps[:, :], rope_sb[:, 0, :], ALU.mult).then_inc(v_cos, 1)

            def mixer_sin(b):
                dve.wait_ge(vs_up, b + 1)
                V.tensor_tensor(vb[:, :], aux_ps[:, :], rope_sb[:, 1, :], ALU.mult).then_inc(v_sin, 1)

            def mixer_scan(b):
                dve.wait_ge(alpha_exp, b + 1)
                V.memset(first_of(alpha), 0.0).then_inc(alpha_done, 1)
                dve.wait_ge(alpha_done, b + 1)
                dve.wait_ge(u_ready, b + 1)
                V.tensor_tensor_scan(local[:, :], alpha[:, :], u[:, :], 0.0, ALU.mult, ALU.add).then_inc(local_done, 1)
                dve.wait_ge(local_done, b + 1)
                dve.wait_ge(small_exp, b + 1)
                V.tensor_tensor_scan(carry[:, 1:NCH], last_of(local)[:, 0:NCH - 1], small_e[:, 1, 1:NCH], 0.0,
                                     ALU.add, ALU.mult).then_inc(carry_done, 1)
                dve.wait_ge(carry_done, b + 1)
                V.tensor_tensor(carry_p[:, 1:NCH], carry[:, 1:NCH], small_e[:, 0, 1:NCH],
                                ALU.mult).then_inc(carry_scaled, 1)
                dve.wait_ge(carry_scaled, b + 1)
                V.tensor_tensor(first_of(u)[:, 1:NCH], first_of(u)[:, 1:NCH], carry_p[:, 1:NCH],
                                ALU.add).then_inc(u_seeded, 1)
                dve.wait_ge(u_seeded, b + 1)
                if b:
                    dve.wait_ge(heads_up, b)
                V.tensor_tensor_scan(final[:, :], alpha[:, :], u[:, :], 0.0, ALU.mult, ALU.add).then_inc(final_done, 1)

            def mixer_gated(b):
                dve.wait_ge(gate_tanh, b + 1)
                dve.wait_ge(heads_up, b + 1)
                if b:
                    dve.wait_ge(out_up, b)
                V.scalar_tensor_tensor(gated[:, :], gate_t[:, :], 1.0, aux_ps[:, :],
                                       ALU.add, ALU.mult).then_inc(gated_done, 1)

            def mixer_add(b):
                dve.wait_ge(out_up, b + 1)
                dve.wait_ge(x_plus_h, b + 1)
                xb = xt[:, b, :, :].rearrange("p t d -> p (t d)")
                V.tensor_tensor(xb, aux_ps[:, :], xb, ALU.add).then_inc(x_mixed, 1)

            pass_stats(0)
            pass_normalise(0)
            dve.wait_ge(zwide_up, 1)
            V.tensor_copy(zsum_wide[:, :], y_ps[:, 0:P]).then_inc(zwide_ready, 1)
            route(0)
            pass_stats(1)
            split_z(0)
            coefficients(0)
            dve.wait_ge(proj_in, 16)
            flat = proj_sb[:, :, :].rearrange("p k n -> p (k n)")
            V.tensor_scalar(flat, flat, 0.5, None, ALU.mult).then_inc(made_proj, 1)
            dve.wait_ge(made_ident, 2)
            dve.wait_ge(vecs_in, 16)
            V.tensor_reduce(head_eye[:, :], ident[:, :].rearrange("p (h d) -> p d h", d=DH), AX_X,
                            ALU.add).then_inc(made_proj, 1)
            dve.wait_ge(made_proj, 2)
            V.tensor_tensor(mix_sb[:, :, :], head_eye[:, :].unsqueeze(1).broadcast_to([P, H, DH]),
                            mix_col.unsqueeze(2).broadcast_to([P, H, DH]), ALU.mult).then_inc(made_mix, 1)
            split_w1(0)
            pass_normalise(1)
            scale_w2(0)
            out_bias(0)
            dve.wait_ge(proj_hi_ready, 1)
            V.tensor_tensor(proj_lo[:, :, :], proj_sb[:, 0:4, :], proj_hi[:, :, :].bitcast(F32),
                            ALU.subtract).then_inc(made_proj, 1)
            dve.wait_ge(made_const, 8)
            dve.wait_ge(rope_in, 16)
            before, after = BEFORE["dve"], AFTER["dve"]
            for tick in range(LAST):
                for q in before_pass(tick, before["stats"], 2):
                    pass_stats(q)
                for q in before_pass(tick, before["normalise"], 2):
                    pass_normalise(q)
                for q in after_pass(tick, after["update"]):
                    update_x(q)
                for b in mixer_at(tick, after["stats"]):
                    mixer_stats(b)
                for q in before_pass(tick, before["widen"]):
                    widen_sum(q)
                for q in before_pass(tick, before["split_z"]):
                    split_z(q)
                for q in before_pass(tick, before["route"]):
                    route(q)
                for q in before_pass(tick, before["coef"]):
                    coefficients(q)
                for q in before_pass(tick, before["split_w1"]):
                    split_w1(q)
                for q in before_pass(tick, before["scale_w2"]):
                    scale_w2(q)
                for q in before_pass(tick, before["bias"]):
                    out_bias(q)
                for b in mixer_at(tick, after["normalise"]):
                    mixer_normalise(b)
                for b in mixer_at(tick, after["h"]):
                    mixer_h(b)
                for b in mixer_at(tick, after["conv"]):
                    mixer_conv(b)
                for b in mixer_at(tick, after["silu"]):
                    mixer_silu(b)
                for b in mixer_at(tick, after["silu_lo"]):
                    mixer_silu_lo(b)
                for b in mixer_at(tick, after["cos"]):
                    mixer_cos(b)
                for b in mixer_at(tick, after["sin"]):
                    mixer_sin(b)
                for b in mixer_at(tick, after["decay"]):
                    mixer_decay(b)
                for b in mixer_at(tick, after["carry"]):
                    mixer_carry_decay(b)
                for b in mixer_at(tick, after["u"]):
                    mixer_input(b)
                for b in mixer_at(tick, after["scan"]):
                    mixer_scan(b)
                for b in mixer_at(tick, after["gated"]):
                    mixer_gated(b)
                for b in mixer_at(tick, after["add"]):
                    mixer_add(b)


def kernel(L0_attn_x, L0_attn_norm_scale, L0_attn_conv_w, L0_attn_conv_b, L0_attn_in_proj_w, L0_attn_dt_bias,
           L0_attn_head_mix, L0_attn_out_proj_w, L0_ffn_gate_w, L0_ffn_w1, L0_ffn_b1, L0_ffn_w2, L0_ffn_b2):
    import numpy as np
    import concourse.bacc as bacc
    from concourse.bass_utils import run_bass_kernel_spmd

    def arr(a):
        return np.ascontiguousarray(np.asarray(a))

    x = arr(L0_attn_x)
    B, N, D = x.shape
    H = L0_attn_head_mix.shape[0]
    dh = D // H
    E, _, F = L0_ffn_w1.shape
    ft = F // D
    w2 = arr(L0_ffn_w2).reshape(E, ft, D, D).transpose(0, 2, 1, 3).reshape(E, D, F)
    b1 = arr(L0_ffn_b1).reshape(E, ft, D).transpose(0, 2, 1)
    b2 = arr(L0_ffn_b2)[:, :, None]
    wpack = np.concatenate([arr(L0_ffn_w1), b1, w2, b2], axis=2)
    win = arr(L0_attn_in_proj_w)
    swapped = win[:, D:2 * D].reshape(D, H, 2, dh // 2)[:, :, ::-1, :].reshape(D, D)
    proj = np.concatenate([win[:, :2 * D], swapped, win[:, 2 * D:], arr(L0_attn_out_proj_w)], axis=1)
    vecs = np.concatenate([arr(L0_attn_conv_w).reshape(D, -1), arr(L0_attn_conv_b)[:, None],
                           arr(L0_attn_dt_bias)[:, None], arr(L0_attn_norm_scale)[:, None],
                           np.repeat(arr(L0_attn_head_mix), dh, axis=0)], axis=1)
    inv = (1.0 / np.float32(10000.0) ** (np.arange(0, dh, 2, dtype=np.float32) / np.float32(dh))).astype(np.float32)
    ang = (np.arange(N, dtype=np.float32)[None, :] * inv[:, None]).astype(np.float32).astype(np.float64)
    cos, sin = np.cos(ang), np.sin(ang)
    rope = np.stack([np.tile(np.concatenate([cos, cos]), (H, 1)),
                     np.tile(np.concatenate([-sin, sin]), (H, 1))]).astype(np.float32)

    ins = {"x_dram": x, "wpack_dram": wpack, "gate_w_dram": arr(L0_ffn_gate_w), "proj_dram": proj,
           "vecs_dram": vecs, "rope_dram": rope}
    from concourse import mybir as mb
    nc = bacc.Bacc("TRN2", target_bir_lowering=False, num_devices=1)
    aps = []
    for name in list(ins):
        a = ins[name] = np.ascontiguousarray(ins[name])
        aps.append(nc.dram_tensor(name, a.shape, mb.dt.from_np(a.dtype), kind="ExternalInput").ap())
    res = nc.dram_tensor("out_dram", x.shape, mb.dt.float32, kind="ExternalOutput").ap()
    macaron_kernel(nc, *aps, res)
    r = run_bass_kernel_spmd(nc, [ins], core_ids=[0])
    return r.results[0]["out_dram"]
```

```python
from contextlib import ExitStack

import concourse.bass as bass
from concourse import mybir

ALU = mybir.AluOpType
ACT = mybir.ActivationFunctionType
F32 = mybir.dt.float32
F32R = mybir.dt.float32r
U32 = mybir.dt.uint32
AX_X = mybir.AxisListType.X

P = 128
HALF = 512
CHUNK = 32
LN_EPS, RMS_EPS = 1e-5, 1e-6
XN_MAX = 60000.0
DT_MIN, DT_MAX = 0.001, 2.0
DECAY_MAX, CUM_DECAY_MAX = 20.0, 80.0

TICKS = 4
SLOT = {"down": 7, "down_parts": 9, "hi": 1, "lo": 6, "parts": 0, "parts_alone": 3, "parts_first": 2}
BEFORE = {
    "pe": {"norm": 10, "route": 14},
    "act": {"turn": 8, "tanh": 24, "split_w1": 20, "split_w2": 28, "logits": 9},
    "dve": {"stats": 0, "normalise": 9, "widen": 10, "split_z": 22, "route": 15, "coef": 26,
            "split_w1": 24, "bias": 31, "scale_w2": 31},
    "pool": {"rstd": 2},
    "sp": {"load": 15},
}
AFTER = {
    "pe": {"turn_y": 4, "norm": 16, "dt": 31, "v": 32, "vs": 35, "gate": 51, "heads": 59, "out": 60},
    "act": {"out": 2, "scale": 16, "silu": 21, "dt": 30, "decay": 37, "gate": 51, "silu_hi": 25, "h": 20,
            "tap": 16},
    "dve": {"update": 8, "stats": 10, "normalise": 13, "silu": 25, "cos": 32, "sin": 37, "decay": 32,
            "carry": 37, "u": 42, "scan": 46, "gated": 57, "add": 62, "silu_lo": 27, "clip": 19,
            "conv1": 22, "conv2": 22, "conv3": 22, "dstep": 37, "u2": 42, "scan2": 53},
    "pool": {"rms": 30, "residual": 41},
    "sp": {"store": 8},
}


def macaron_kernel(nc, x, wpack, gate_w, proj, vecs, rope, out):
    B, N, D = x.shape
    E = gate_w.shape[1]
    F = (wpack.shape[2] - 1) // (2 + 1 / P)
    F = int(round(F))
    FT = F // P
    NT = N // P
    NCH = N // CHUNK
    TOP = 2
    SLOTS = TOP * FT
    PASSES = 2 * B
    PACK = wpack.shape[2]
    B1_AT, W2_AT, B2_AT = F, F + FT, 2 * F + FT
    HBUF = 4
    WARM = 14
    POOL_STEPS = 5
    assert D == P and N == 2 * HALF and PACK == 2 * F + FT + 1
    H = vecs.shape[1] - 4 - 3
    DH = D // H

    with ExitStack() as ctx:
        def sb(name, shape, dt=F32):
            return ctx.enter_context(nc.sbuf_tensor(name, shape, dt))

        def sem(name):
            return ctx.enter_context(nc.semaphore(name))

        hid_ps = ctx.enter_context(nc.psum_tensor("hid_ps", [P, 2, N], F32))
        y_ps = ctx.enter_context(nc.psum_tensor("y_ps", [P, N], F32))
        aux_ps = ctx.enter_context(nc.psum_tensor("aux_ps", [P, N], F32))

        xt = sb("xt", [P, B, NT, D])
        ident = sb("ident", [P, P])
        ones = sb("ones", [P, P])
        neg_half = sb("neg_half", [P, 2, NT])
        gate_sb = sb("gate_sb", [P, E])
        proj_sb = sb("proj_sb", [P, 5, P])
        vec_sb = sb("vec_sb", [P, 7 + H])
        conv_w, conv_b = vec_sb[:, 0:4], vec_sb[:, 4:5]
        dt_bias, norm_scale, mix_col = vec_sb[:, 5:6], vec_sb[:, 6:7], vec_sb[:, 7:7 + H]
        rope_sb = sb("rope_sb", [P, 2, N])
        head_eye = sb("head_eye", [P, DH])
        mix_sb = sb("mix_sb", [P, H, DH])
        in_chunk = sb("in_chunk", [P, N])
        cum_cap = sb("cum_cap", [P, NCH])
        w_sb = sb("w_sb", [P, 2, TOP, PACK])
        f_stat = sb("f_stat", [P, NT, 6])
        f_mv = sb("f_mv", [P, NT, 2])
        f_ve = sb("f_ve", [P, NT])
        f_rstd = sb("f_rstd", [P, NT])
        f_tok = sb("f_tok", [P, NT, D])
        z_hi, z_lo = sb("z_hi", [P, 2, N], F32R), sb("z_lo", [P, 2, N], F32R)
        w1_hi, w1_lo = sb("w1_hi", [P, 2, TOP, F], F32R), sb("w1_lo", [P, 2, TOP, F], F32R)
        w2_hi, w2_lo = sb("w2_hi", [P, 2, TOP, F], F32R), sb("w2_lo", [P, 2, TOP, F], F32R)
        zsum = sb("zsum", [P, 1])
        zsum_wide = sb("zsum_wide", [P, P])
        logit = sb("logit", [P, E])
        top_v = sb("top_v", [P, 8])
        top_i = sb("top_i", [P, 8], U32)
        top_d = sb("top_d", [P, 1])
        top_t = sb("top_t", [P, 1])
        coef = sb("coef", [P, 2, TOP])
        bias2a = sb("bias2a", [P, 1])
        bias2 = sb("bias2", [P, 2, 1])
        hid = sb("hid", [P, HBUF, N])
        hid_hi, hid_lo = sb("hid_hi", [P, 2, N], F32R), sb("hid_lo", [P, 2, N], F32R)
        yt = sb("yt", [P, N])
        m_stat = sb("m_stat", [P, NT, 6])
        m_mv = sb("m_mv", [P, NT, 2])
        m_var = sb("m_var", [P, 2, NT])
        m_inv = sb("m_inv", [P, 2, NT])
        m_rms = sb("m_rms", [P, NT])
        m_h = sb("m_h", [P, NT, D])
        m_tok = sb("m_tok", [P, NT, D])
        PAD = 3
        xs = sb("xs", [P, PAD + N])
        xc = sb("xc", [P, N])
        silu = sb("silu", [P, N])
        silu_hi, silu_lo = sb("silu_hi", [P, N], F32R), sb("silu_lo", [P, N], F32R)
        proj_hi, proj_lo = sb("proj_hi", [P, 4, P], F32R), sb("proj_lo", [P, 4, P], F32R)
        dt_t = sb("dt_t", [P, N])
        decay = sb("decay", [P, N])
        dstep = sb("dstep", [P, N])
        alpha = sb("alpha", [P, N])
        small = sb("small", [P, 2, NCH])
        small_e = sb("small_e", [P, 2, NCH])
        cumd = sb("cumd", [P, NCH])
        ncd = sb("ncd", [P, NCH])
        carry = sb("carry", [P, NCH])
        carry_p = sb("carry_p", [P, NCH])
        va = sb("va", [P, N])
        vb = sb("vb", [P, N])
        u = sb("u", [P, N])
        state = sb("state", [P, N])
        gated = sb("gated", [P, N])

        def first_of(t):
            return t[:, :].rearrange("p (c t) -> p c t", t=CHUNK)[:, :, 0]

        def last_of(t):
            return t[:, :].rearrange("p (c t) -> p c t", t=CHUNK)[:, :, CHUNK - 1]

        x_in = [sem(f"x_in{b}") for b in range(B)]
        x_in_tail = sem("x_in_tail")
        proj_in, rope_in, small_in, vecs_in = sem("proj_in"), sem("rope_in"), sem("small_in"), sem("vecs_in")
        w1_head_in, w1_head_hi, w1_head_lo = sem("w1_head_in"), sem("w1_head_hi"), sem("w1_head_lo")
        w1_in = [[sem(f"w1_in{i}_{k}") for k in range(TOP)] for i in range(2)]
        w2_in = [sem(f"w2_in{i}") for i in range(2)]
        out_done = sem("out_done")
        made_ident, made_const, made_proj, made_mix = (
            sem("made_ident"), sem("made_const"), sem("made_proj"), sem("made_mix"))
        f_stats_step, f_aggr_done = sem("f_stats_step"), sem("f_aggr_done")
        f_var_eps, f_rstd_done, f_norm_done = sem("f_var_eps"), sem("f_rstd_done"), sem("f_norm_done")
        f_rstd_head, zwide_up = sem("f_rstd_head"), sem("zwide_up")
        f_turned, zt_ready, zwide_ready = sem("f_turned"), sem("zt_ready"), sem("zwide_ready")
        logits_up, logits_read, top_ready = sem("logits_up"), sem("logits_read"), sem("top_ready")
        index_ready, diff_ready, tanh_ready, coef_ready = (
            sem("index_ready"), sem("diff_ready"), sem("tanh_ready"), sem("coef_ready"))
        zhi_ready, zlo_ready = sem("zhi_ready"), sem("zlo_ready")
        w1_hi_ready, w1_lo_ready = sem("w1_hi_ready"), sem("w1_lo_ready")
        w2_hi_ready, w2_lo_ready = sem("w2_hi_ready"), sem("w2_lo_ready")
        hid_hi_ready, hid_lo_ready = sem("hid_hi_ready"), sem("hid_lo_ready")
        bias2a_ready, bias2_ready, w2_scaled = sem("bias2a_ready"), sem("bias2_ready"), sem("w2_scaled")
        hid_up, hid_ready, hid_used = sem("hid_up"), sem("hid_ready"), sem("hid_used")
        yt_ready, y_turned, x_updated = sem("yt_ready"), sem("y_turned"), sem("x_updated")
        m_stats_step, m_aggr_done, m_pool_step = sem("m_stats_step"), sem("m_aggr_done"), sem("m_pool_step")
        m_h_done, m_norm_done, x_plus_h = sem("m_h_done"), sem("m_norm_done"), sem("x_plus_h")
        m_turned, xs_ready, xs_clipped, conv_step = (
            sem("m_turned"), sem("xs_ready"), sem("xs_clipped"), sem("conv_step"))
        silu_tanh, silu_done = sem("silu_tanh"), sem("silu_done")
        silu_hi_done, silu_lo_done, proj_hi_ready = sem("silu_hi_done"), sem("silu_lo_done"), sem("proj_hi_ready")
        dt_up, dt_exp, dt_ln, dt_done = sem("dt_up"), sem("dt_exp"), sem("dt_ln"), sem("dt_done")
        decay_sum, decay_done, dstep_done, first_done = (
            sem("decay_sum"), sem("decay_done"), sem("dstep_done"), sem("first_done"))
        cumd_done, ncd_done, small_done = sem("cumd_done"), sem("ncd_done"), sem("small_done")
        alpha_exp, small_exp, alpha_done = sem("alpha_exp"), sem("small_exp"), sem("alpha_done")
        v_up, v_cos, vs_up, v_sin, v_rot, u_ready = (
            sem("v_up"), sem("v_cos"), sem("vs_up"), sem("v_sin"), sem("v_rot"), sem("u_ready"))
        local_done, carry_done, carry_scaled, u_seeded, final_done = (
            sem("local_done"), sem("carry_done"), sem("carry_scaled"), sem("u_seeded"), sem("final_done"))
        gate_up, gate_tanh, heads_up, gated_done, out_up, x_mixed = (
            sem("gate_up"), sem("gate_tanh"), sem("heads_up"), sem("gated_done"), sem("out_up"), sem("x_mixed"))

        PERIOD = TICKS * SLOTS
        LAST = PASSES * PERIOD + max(AFTER[e][k] for e, k in (("pe", "turn_y"), ("dve", "update"), ("sp", "store"))) + 1

        def split_of(q):
            return SLOT["parts_first"] if q == 0 else SLOT["parts_alone"] if q > B else SLOT["parts"]

        def by_parts(slot):
            return slot % FT < split_of(slot // SLOTS)

        def split_slots(slot):
            return sum(by_parts(s) for s in range(slot + 1))

        def after_pass(tick, offset):
            return [q for q in range(PASSES) if tick == PERIOD * (q + 1) + offset]

        def mixer_at(tick, offset):
            return [b for b in after_pass(tick, offset) if b < B]

        def before_pass(tick, offset, first=1):
            q, r = divmod(tick - offset, PERIOD)
            return [q + 1] if r == 0 and first <= q + 1 < PASSES else []

        def parts_of(q, n):
            return [slice(0, n)] if q < PASSES - 1 else [slice(0, n // 2), slice(n // 2, n)]

        def slot_at(tick, offset, offset_by_parts=None):
            if offset_by_parts is None:
                offset_by_parts = offset
            return [s for s in range(PASSES * SLOTS)
                    if tick == TICKS * s + (offset_by_parts if by_parts(s) else offset)]

        def split_at(tick, offset):
            return [s for s in slot_at(tick, offset) if by_parts(s)]

        block = ctx.enter_context(nc.Block())

        @block.sync
        def _(sp):
            def load_x(b):
                sp.dma_start(xt[:, b, :, :], x[b].rearrange("(t p) d -> p t d", p=P)).then_inc(x_in[b], 16)

            def load_experts(q):
                if q >= 2:
                    sp.wait_ge(hid_used, SLOTS * (q - 1))
                    sp.wait_ge(bias2_ready, q - 1)
                sp.wait_ge(index_ready, q + 1)
                src = []
                for k in range(TOP):
                    e = sp.value_load(top_i[0:1, k:k + 1], min_val=0, max_val=E - 1)
                    src.append(wpack[bass.ds(e, 1), :, :].rearrange("e p n -> p (e n)"))
                    head = P if q == 0 and k == 0 else 0
                    if head:
                        sp.dma_start(w_sb[:, 0, 0, 0:head], src[k][:, 0:head]).then_inc(w1_head_in, 16)
                    sp.dma_start(w_sb[:, q % 2, k, head:W2_AT], src[k][:, head:W2_AT]).then_inc(w1_in[q % 2][k], 16)
                for k in range(TOP):
                    sp.dma_start(w_sb[:, q % 2, k, W2_AT:], src[k][:, W2_AT:]).then_inc(w2_in[q % 2], 16)

            x0 = x[0].rearrange("(t p) d -> p t d", p=P)
            sp.dma_start(xt[:, 0, 0:NT // 2, :], x0[:, 0:NT // 2, :]).then_inc(x_in[0], 16)
            sp.dma_start(gate_sb[:, :], gate_w).then_inc(small_in, 16)
            load_x(1)
            load_experts(0)
            load_x(2)
            load_x(3)
            for tick in range(LAST):
                for q in after_pass(tick, AFTER["sp"]["store"]):
                    if q >= B:
                        for i, tiles in enumerate(parts_of(q, NT)):
                            sp.wait_ge(x_updated, 2 * q + (2 if q < PASSES - 1 else 1 + i))
                            sp.dma_start(out[q - B].rearrange("(t p) d -> p t d", p=P)[:, tiles, :],
                                         xt[:, q - B, tiles, :]).then_inc(out_done, 16)
                for q in before_pass(tick, BEFORE["sp"]["load"]):
                    load_experts(q)
            sp.wait_ge(out_done, 16 * (B + 1))

        @block.gpsimd
        def _(pool):
            nc.gpsimd.memset(ident[:, :], 0.0).then_inc(made_ident, 1)
            pool.wait_ge(made_ident, 1)
            nc.gpsimd.affine_select(out=ident[:, :], in_=ident[:, :], compare_op=ALU.not_equal, fill=1.0,
                                    base=0, pattern=[[-1, P]], channel_multiplier=1).then_inc(made_ident, 1)
            nc.gpsimd.memset(neg_half[:, :, :], -0.5).then_inc(made_const, 1)
            nc.gpsimd.memset(ones[:, :], 1.0).then_inc(made_const, 1)
            nc.gpsimd.memset(xs[:, 0:PAD], 0.0).then_inc(made_const, 1)
            nc.gpsimd.memset(dstep[:, 0:1], 0.0).then_inc(made_const, 1)
            nc.gpsimd.memset(small[:, 1, 0:1], 0.0).then_inc(made_const, 1)
            nc.gpsimd.memset(cum_cap[:, :], CUM_DECAY_MAX).then_inc(made_const, 1)
            pool.dma_start(proj_sb[:, :, :], proj.rearrange("p (k n) -> p k n", n=P)).then_inc(proj_in, 16)
            pool.dma_start(rope_sb[:, :, :], rope.rearrange("k p n -> p k n")).then_inc(rope_in, 16)

            def rstd_of(q, tiles, step, done):
                nc.gpsimd.tensor_scalar(f_ve[:, tiles], f_mv[:, tiles, 1], LN_EPS, None, ALU.add).then_inc(f_var_eps, 1)
                pool.wait_ge(f_var_eps, step)
                nc.gpsimd.tensor_tensor(f_rstd[:, tiles], f_ve[:, tiles], neg_half[:, 0, tiles],
                                        ALU.pow).then_inc(done, 1)

            def pass_rstd(q):
                if q == 0:
                    pool.wait_ge(f_aggr_done, NT // 2)
                    rstd_of(q, slice(0, NT // 2), 1, f_rstd_head)
                    pool.wait_ge(f_aggr_done, NT)
                    rstd_of(q, slice(NT // 2, NT), 2, f_rstd_done)
                else:
                    pool.wait_ge(f_aggr_done, NT * (q + 1))
                    pool.wait_ge(f_norm_done, NT * q)
                    rstd_of(q, slice(0, NT), q + 2, f_rstd_done)

            def mixer_rms(b):
                pool.wait_ge(m_aggr_done, NT * (b + 1))
                if b:
                    pool.wait_ge(m_h_done, NT * b)
                nc.gpsimd.tensor_scalar(m_var[:, 0, :], m_mv[:, :, 1], LN_EPS, None, ALU.add).then_inc(m_pool_step, 1)
                nc.gpsimd.tensor_scalar(m_var[:, 1, :], m_mv[:, :, 1], 1.0 + RMS_EPS, LN_EPS * RMS_EPS,
                                        ALU.mult, ALU.add).then_inc(m_pool_step, 1)
                pool.wait_ge(m_pool_step, POOL_STEPS * b + 2)
                nc.gpsimd.tensor_tensor(m_inv[:, :, :], m_var[:, :, :], neg_half[:, :, :],
                                        ALU.pow).then_inc(m_pool_step, 1)
                pool.wait_ge(m_pool_step, POOL_STEPS * b + 3)
                nc.gpsimd.tensor_tensor(m_rms[:, :], m_var[:, 1, :], m_inv[:, 1, :], ALU.mult).then_inc(m_pool_step, 1)
                pool.wait_ge(m_pool_step, POOL_STEPS * b + 4)
                nc.gpsimd.tensor_tensor(m_rms[:, :], m_rms[:, :], m_inv[:, 0, :], ALU.mult).then_inc(m_pool_step, 1)

            def mixer_residual(b):
                pool.wait_ge(m_h_done, NT * (b + 1))
                xb = xt[:, b, :, :]
                nc.gpsimd.tensor_tensor(xb, xb, m_h[:, :, :], ALU.add).then_inc(x_plus_h, 1)

            pool.wait_ge(made_const, 2)
            pass_rstd(0)
            nc.gpsimd.memset(in_chunk[:, :], 1.0).then_inc(made_const, 1)
            pool.wait_ge(made_const, 7)
            nc.gpsimd.memset(first_of(in_chunk), 0.0).then_inc(made_const, 1)
            pass_rstd(1)
            before, after = BEFORE["pool"], AFTER["pool"]
            for tick in range(LAST):
                for q in before_pass(tick, before["rstd"], 2):
                    pass_rstd(q)
                for b in mixer_at(tick, after["rms"]):
                    mixer_rms(b)
                for b in mixer_at(tick, after["residual"]):
                    mixer_residual(b)

        @block.scalar
        def _(act):
            def turn_z(q):
                act.wait_ge(f_turned, q + 1)
                if q:
                    act.wait_ge(zwide_ready, q)
                f_feat = f_tok[:, :, :].rearrange("p t d -> p (t d)")
                nc.scalar.activation(f_feat, aux_ps[:, :], ACT.Copy, accum_out=zsum[:, :]).then_inc(zt_ready, 1)
                act.wait_ge(zt_ready, q + 1)
                if q >= 2:
                    act.wait_ge(hid_up, SLOTS * (q - 1))
                nc.scalar.activation(z_hi[:, q % 2, :], f_feat, ACT.Copy).then_inc(zhi_ready, 1)

            def read_logits(q):
                act.wait_ge(logits_up, q + 1)
                if q:
                    act.wait_ge(diff_ready, q)
                logits = aux_ps[:, 0:E] if q else y_ps[:, HALF:HALF + E]
                nc.scalar.activation(logit[:, :], logits, ACT.Copy).then_inc(logits_read, 1)

            def top_tanh(q):
                act.wait_ge(diff_ready, q + 1)
                nc.scalar.activation(top_t[:, :], top_d[:, :], ACT.Tanh, scale=0.5 / N).then_inc(tanh_ready, 1)

            def split_w1(q):
                if q >= 2:
                    act.wait_ge(hid_up, SLOTS * (q - 1))
                for k in range(TOP):
                    head = P if q == 0 and k == 0 else 0
                    if head:
                        act.wait_ge(w1_head_in, 16)
                        nc.scalar.activation(w1_hi[:, 0, 0, 0:head], w_sb[:, 0, 0, 0:head],
                                             ACT.Copy).then_inc(w1_head_hi, 1)
                    act.wait_ge(w1_in[q % 2][k], 16 * (q // 2 + 1))
                    nc.scalar.activation(w1_hi[:, q % 2, k, head:], w_sb[:, q % 2, k, head:F],
                                         ACT.Copy).then_inc(w1_hi_ready, 1)

            def gelu(slot):
                q, t = divmod(slot, SLOTS)
                act.wait_ge(hid_up, slot + 1)
                if slot >= HBUF:
                    act.wait_ge(hid_used, slot - HBUF + 1)
                k, f = divmod(t, FT)
                bias = w_sb[:, q % 2, k, B1_AT + f:B1_AT + f + 1]
                nc.scalar.activation(hid[:, slot % HBUF, :], hid_ps[:, slot % 2, :], ACT.Gelu,
                                     bias=bias).then_inc(hid_ready, 1)

            def split_hid(slot):
                act.wait_ge(hid_ready, slot + 1)
                if slot >= 2:
                    act.wait_ge(hid_used, slot - 1)
                nc.scalar.activation(hid_hi[:, slot % 2, :], hid[:, slot % HBUF, :],
                                     ACT.Copy).then_inc(hid_hi_ready, 1)

            def split_w2(q):
                act.wait_ge(w2_in[q % 2], 16 * TOP * (q // 2 + 1))
                act.wait_ge(coef_ready, TOP * (q + 1))
                if q >= 2:
                    act.wait_ge(hid_used, SLOTS * (q - 1))
                n = split_of(q) * P
                for k in range(TOP if n else 0):
                    nc.scalar.activation(w2_hi[:, q % 2, k, 0:n], w_sb[:, q % 2, k, W2_AT:W2_AT + n], ACT.Copy,
                                         scale=coef[:, q % 2, k:k + 1]).then_inc(w2_hi_ready, 1)

            def pass_out(q):
                act.wait_ge(bias2_ready, q + 1)
                if q:
                    act.wait_ge(y_turned, 2 * q)
                for i, cols in enumerate(parts_of(q, N)):
                    act.wait_ge(hid_used, SLOTS * (q + 1) + i)
                    nc.scalar.activation(yt[:, cols], y_ps[:, cols], ACT.Identity,
                                         bias=bias2[:, q % 2, :]).then_inc(yt_ready, 1)

            def mixer_scale(b):
                act.wait_ge(m_turned, b + 1)
                if b:
                    act.wait_ge(conv_step, 4 * b)
                nc.scalar.activation(xs[:, PAD:], aux_ps[:, :], ACT.Copy, scale=norm_scale).then_inc(xs_ready, 1)

            def mixer_h(b):
                act.wait_ge(m_norm_done, NT * (b + 1))
                act.wait_ge(m_pool_step, POOL_STEPS * (b + 1))
                if b:
                    act.wait_ge(x_plus_h, b)
                for t in range(NT):
                    nc.scalar.activation(m_h[:, t, :], m_tok[:, t, :], ACT.Copy,
                                         scale=m_rms[:, t:t + 1]).then_inc(m_h_done, 1)

            def mixer_tap(b):
                act.wait_ge(xs_clipped, b + 1)
                if b:
                    act.wait_ge(silu_done, b)
                nc.scalar.activation(xc[:, :], xs[:, 0:N], ACT.Identity, bias=conv_b,
                                     scale=conv_w[:, 0:1]).then_inc(conv_step, 1)

            def mixer_silu(b):
                act.wait_ge(conv_step, 4 * (b + 1))
                if b:
                    act.wait_ge(silu_lo_done, b)
                nc.scalar.activation(silu[:, :], xc[:, :], ACT.Tanh, scale=0.5).then_inc(silu_tanh, 1)

            def mixer_silu_hi(b):
                act.wait_ge(silu_done, b + 1)
                if b:
                    act.wait_ge(gate_up, b)
                nc.scalar.activation(silu_hi[:, :], silu[:, :], ACT.Copy).then_inc(silu_hi_done, 1)

            def mixer_dt(b):
                nc.scalar.preload_act_table_set("natural_log_exp_and_others")
                act.wait_ge(dt_up, b + 1)
                if b:
                    act.wait_ge(u_ready, b)
                nc.scalar.activation(dt_t[:, :], aux_ps[:, :], ACT.Exp, bias=dt_bias).then_inc(dt_exp, 1)
                act.wait_ge(dt_exp, b + 1)
                nc.scalar.activation(dt_t[:, :], dt_t[:, :], ACT.Ln, bias=1.0).then_inc(dt_ln, 1)
                nc.scalar.preload_act_table_set("gelu_and_others")

            def mixer_decay(b):
                nc.scalar.preload_act_table_set("natural_log_exp_and_others")
                act.wait_ge(dstep_done, b + 1)
                if b:
                    act.wait_ge(final_done, b)
                nc.scalar.activation(alpha[:, :], dstep[:, :], ACT.Exp).then_inc(alpha_exp, 1)
                act.wait_ge(first_done, b + 1)
                act.wait_ge(small_done, b + 1)
                nc.scalar.activation(small_e[:, :, :], small[:, :, :], ACT.Exp).then_inc(small_exp, 1)
                nc.scalar.preload_act_table_set("gelu_and_others")

            def mixer_gate(b):
                act.wait_ge(gate_up, b + 1)
                if b:
                    act.wait_ge(out_up, 2 * b)
                nc.scalar.activation(gated[:, :], aux_ps[:, :], ACT.Tanh, scale=0.5).then_inc(gate_tanh, 1)

            x0 = x[0].rearrange("(t p) d -> p t d", p=P)
            act.dma_start(xt[:, 0, NT // 2:, :], x0[:, NT // 2:, :]).then_inc(x_in_tail, 16)
            act.dma_start(vec_sb[:, :], vecs).then_inc(vecs_in, 16)
            nc.scalar.preload_act_table_set("gelu_and_others")
            read_logits(0)
            turn_z(0)
            top_tanh(0)
            split_w1(0)
            act.wait_ge(vecs_in, 16)
            act.wait_ge(made_const, 6)
            before, after = BEFORE["act"], AFTER["act"]
            for tick in range(LAST):
                for slot in slot_at(tick, 0):
                    gelu(slot)
                if tick == 1:
                    split_w2(0)
                if tick == 3 * TICKS:
                    act.wait_ge(made_proj, 1)
                    nc.scalar.activation(proj_hi[:, :, :], proj_sb[:, 0:4, :], ACT.Copy).then_inc(proj_hi_ready, 1)
                for slot in split_at(tick, SLOT["hi"]):
                    split_hid(slot)
                for b in mixer_at(tick, after["silu"]):
                    mixer_silu(b)
                for q in after_pass(tick, after["out"]):
                    pass_out(q)
                for q in before_pass(tick, before["turn"]):
                    turn_z(q)
                for q in before_pass(tick, before["logits"]):
                    read_logits(q)
                for q in before_pass(tick, before["tanh"]):
                    top_tanh(q)
                for q in before_pass(tick, before["split_w1"]):
                    split_w1(q)
                for q in before_pass(tick, before["split_w2"]):
                    split_w2(q)
                for b in mixer_at(tick, after["scale"]):
                    mixer_scale(b)
                for b in mixer_at(tick, after["h"]):
                    mixer_h(b)
                for b in mixer_at(tick, after["tap"]):
                    mixer_tap(b)
                for b in mixer_at(tick, after["silu_hi"]):
                    mixer_silu_hi(b)
                for b in mixer_at(tick, after["dt"]):
                    mixer_dt(b)
                for b in mixer_at(tick, after["decay"]):
                    mixer_decay(b)
                for b in mixer_at(tick, after["gate"]):
                    mixer_gate(b)

        @block.tensor
        def _(pe):
            def up(slot):
                q, t = divmod(slot, SLOTS)
                k, f = divmod(t, FT)
                if slot == 0:
                    pe.wait_ge(w1_head_hi, 1)
                elif slot == 1 or f == 0:
                    pe.wait_ge(w1_hi_ready, TOP * q + k + 1)
                if t == 0:
                    pe.wait_ge(zhi_ready, q + 1)
                if slot >= 2:
                    pe.wait_ge(hid_ready, slot - 1)
                rows = slice(f * P, (f + 1) * P)
                hi, lo = w1_hi[:, q % 2, k, rows], w1_lo[:, q % 2, k, rows]
                for w, z, first, end in ((hi, z_hi, True, False), (hi, z_lo, False, False), (lo, z_hi, False, True)):
                    if t == 0 and z is z_lo:
                        pe.wait_ge(zlo_ready, q + 1)
                    if slot == 0 and w is lo:
                        pe.wait_ge(w1_head_lo, 1)
                    elif (slot == 1 or f == 0) and w is lo:
                        pe.wait_ge(w1_lo_ready, TOP * q + k + 1)
                    for h in range(2):
                        cols = slice(h * HALF, (h + 1) * HALF)
                        last = nc.tensor.matmul(hid_ps[:, slot % 2, cols], w, z[:, q % 2, cols],
                                                start=first, stop=end)
                last.then_inc(hid_up, 1)

            def down(slot):
                q, t = divmod(slot, SLOTS)
                k, f = divmod(t, FT)
                if f == 0 and by_parts(slot):
                    pe.wait_ge(w2_lo_ready, TOP * sum(split_of(p) > 0 for p in range(q)) + k + 1)
                if f == split_of(q):
                    pe.wait_ge(w2_scaled, TOP * sum(split_of(p) < FT for p in range(q)) + k + 1)
                if t == 0 and q:
                    pe.wait_ge(yt_ready, q)
                if by_parts(slot):
                    rows = slice(f * P, (f + 1) * P)
                    hi, lo = w2_hi[:, q % 2, k, rows], w2_lo[:, q % 2, k, rows]
                    h_hi, h_lo = hid_hi[:, slot % 2, :], hid_lo[:, slot % 2, :]
                    terms = [(hi, h_hi, hid_hi_ready), (lo, h_hi, None), (hi, h_lo, hid_lo_ready)]
                else:
                    pe.wait_ge(hid_ready, slot + 1)
                    w2 = w_sb[:, q % 2, k, W2_AT + f * P:W2_AT + (f + 1) * P]
                    terms = [(w2, hid[:, slot % HBUF, :], None)]
                for i, (wt, src, ready) in enumerate(terms):
                    if ready:
                        pe.wait_ge(ready, split_slots(slot))
                    for half in range(2):
                        cols = slice(half * HALF, (half + 1) * HALF)
                        end = i == len(terms) - 1
                        last = nc.tensor.matmul(y_ps[:, cols], wt, src[:, cols], start=t == 0 and i == 0,
                                                stop=t == SLOTS - 1 and end)
                        if slot == PASSES * SLOTS - 1 and end and half == 0:
                            last.then_inc(hid_used, 1)
                last.then_inc(hid_used, 1)

            last_reader = []

            def take_aux(*reader):
                before = last_reader.pop() if last_reader else None
                last_reader.append(reader)

                def free(half):
                    if before and (half == 0 or before[2] > before[1]):
                        pe.wait_ge(before[0], before[1 + half])
                return free

            def turn(tiles, free, tile_ready, before):
                for t in range(NT):
                    if t % (NT // 2) == 0:
                        free(t // (NT // 2))
                    pe.wait_ge(tile_ready, before + t + 1)
                    last = nc.tensor.transpose(aux_ps[:, t * P:(t + 1) * P], tiles(t), ident[:, :])
                return last

            def pre_norm(q):
                free = take_aux(zt_ready, q + 1, q + 1)
                turn(lambda t: f_tok[:, t, :], free, f_norm_done, NT * q).then_inc(f_turned, 1)

            def pre_route(q):
                pe.wait_ge(zwide_ready, q + 1)
                free = take_aux(logits_read, q + 1, q + 1)
                free(0)
                free(1)
                nc.tensor.matmul(aux_ps[:, 0:E], zsum_wide[:, :], gate_sb[:, :],
                                 start=True, stop=True).then_inc(logits_up, 1)

            def post(q):
                free = take_aux(x_updated, 2 * q + 1, 2 * q + 2)
                pe.wait_ge(yt_ready, q + 1)
                for half in range(2):
                    free(half)
                    if q == PASSES - 1:
                        pe.wait_ge(yt_ready, q + 1 + half)
                    for t in range(half * NT // 2, (half + 1) * NT // 2):
                        cols = slice(t * P, (t + 1) * P)
                        last = nc.tensor.transpose(aux_ps[:, cols], yt[:, cols], ident[:, :])
                    last.then_inc(y_turned, 1)

            def mixer_norm(b):
                free = take_aux(xs_ready, b + 1, b + 1)
                turn(lambda t: m_tok[:, t, :], free, m_norm_done, NT * b).then_inc(m_turned, 1)

            def project_silu(b, w, free, done, by_half):
                if w == 0:
                    pe.wait_ge(silu_hi_done, b + 1)
                    if b == 0:
                        pe.wait_ge(made_proj, 3)
                for half in range(2):
                    free(half)
                    cols = slice(half * HALF, (half + 1) * HALF)
                    for wt, z, first, end in ((proj_hi, silu_hi, True, False), (proj_lo, silu_hi, False, False),
                                              (proj_hi, silu_lo, False, True)):
                        if w == 0 and half == 0 and z is silu_lo:
                            pe.wait_ge(silu_lo_done, b + 1)
                        last = nc.tensor.matmul(aux_ps[:, cols], wt[:, w, :], z[:, cols], start=first, stop=end)
                    if by_half or half == 1:
                        last.then_inc(done, 1)

            def mixer_dt(b):
                project_silu(b, 0, take_aux(dt_exp, b + 1, b + 1), dt_up, False)

            def mixer_v(b):
                project_silu(b, 1, take_aux(v_cos, 2 * b + 1, 2 * b + 2), v_up, True)

            def mixer_vs(b):
                project_silu(b, 2, take_aux(v_sin, 2 * b + 1, 2 * b + 2), vs_up, True)

            def mixer_gate(b):
                project_silu(b, 3, take_aux(gate_tanh, b + 1, b + 1), gate_up, False)

            def mixer_heads(b):
                pe.wait_ge(final_done, b + 1)
                if b == 0:
                    pe.wait_ge(made_mix, 1)
                free = take_aux(gated_done, 2 * b + 1, 2 * b + 2)
                for half in range(2):
                    free(half)
                    cols = slice(half * HALF, (half + 1) * HALF)
                    nc.tensor.matmul(aux_ps[:, cols], mix_sb[:, :, :].rearrange("p m d -> p (m d)"),
                                     state[:, cols], start=True, stop=True).then_inc(heads_up, 1)

            def mixer_out(b):
                free = take_aux(x_mixed, 2 * b + 1, 2 * b + 2)
                for half in range(2):
                    free(half)
                    pe.wait_ge(gated_done, 2 * b + 1 + half)
                    for t in range(half * NT // 2, (half + 1) * NT // 2):
                        cols = slice(t * P, (t + 1) * P)
                        last = nc.tensor.matmul(aux_ps[:, cols], gated[:, cols], proj_sb[:, 4, :],
                                                start=True, stop=True)
                    last.then_inc(out_up, 1)

            pe.wait_ge(made_const, 2)
            for t in range(NT):
                pe.wait_ge(f_norm_done, t + 1)
                last = nc.tensor.matmul(y_ps[:, 0:P], f_tok[:, t, :], ones[:, :], start=t == 0, stop=t == NT - 1)
            last.then_inc(zwide_up, 1)
            pe.wait_ge(small_in, 16)
            pe.wait_ge(zwide_ready, 1)
            nc.tensor.matmul(y_ps[:, HALF:HALF + E], zsum_wide[:, :], gate_sb[:, :],
                             start=True, stop=True).then_inc(logits_up, 1)
            pe.wait_ge(made_ident, 2)
            pre_norm(0)
            for _ in range(WARM):
                nc.tensor.matmul(hid_ps[:, 0, 0:P], ones[:, :], ones[:, :], start=True, stop=True)
            before, after = BEFORE["pe"], AFTER["pe"]
            for tick in range(LAST):
                for slot in slot_at(tick, 0):
                    up(slot)
                for slot in slot_at(tick, SLOT["down"], SLOT["down_parts"]):
                    down(slot)
                for q in after_pass(tick, after["turn_y"]):
                    post(q)
                for q in before_pass(tick, before["norm"]):
                    pre_norm(q)
                for q in before_pass(tick, before["route"]):
                    pre_route(q)
                for b in mixer_at(tick, after["norm"]):
                    mixer_norm(b)
                for b in mixer_at(tick, after["dt"]):
                    mixer_dt(b)
                for b in mixer_at(tick, after["v"]):
                    mixer_v(b)
                for b in mixer_at(tick, after["vs"]):
                    mixer_vs(b)
                for b in mixer_at(tick, after["gate"]):
                    mixer_gate(b)
                for b in mixer_at(tick, after["heads"]):
                    mixer_heads(b)
                for b in mixer_at(tick, after["out"]):
                    mixer_out(b)

        @block.vector
        def _(dve):
            V = nc.vector

            def pass_stats(q):
                b = q % B
                if q < B:
                    dve.wait_ge(x_in[b], 16)
                else:
                    dve.wait_ge(x_mixed, 2 * (b + 1))
                if q:
                    dve.wait_ge(f_rstd_done, q)
                for tiles in (range(0, NT // 2), range(NT // 2, NT)) if q == 0 else (range(NT),):
                    if q == 0 and tiles[0]:
                        dve.wait_ge(x_in_tail, 16)
                    for t in tiles:
                        V.bn_stats(f_stat[:, t, :], xt[:, b, t, :]).then_inc(f_stats_step, 1)
                    for t in tiles:
                        dve.wait_ge(f_stats_step, NT * q + t + 1)
                        V.bn_aggr(f_mv[:, t, :], f_stat[:, t, :]).then_inc(f_aggr_done, 1)

            def pass_normalise(q):
                if q:
                    dve.wait_ge(f_rstd_done, q + 1)
                    dve.wait_ge(zlo_ready, q)
                dve.wait_ge(f_aggr_done, NT * (q + 1))
                for t in range(NT):
                    if q == 0 and t == 0:
                        dve.wait_ge(f_rstd_head, 1)
                    if q == 0 and t == NT // 2:
                        dve.wait_ge(f_rstd_done, 1)
                    V.tensor_scalar(f_tok[:, t, :], xt[:, q % B, t, :], f_mv[:, t, 0:1], f_rstd[:, t:t + 1],
                                    ALU.subtract, ALU.mult).then_inc(f_norm_done, 1)

            def split_z(q):
                dve.wait_ge(zhi_ready, q + 1)
                if q >= 2:
                    dve.wait_ge(hid_up, SLOTS * (q - 1))
                V.tensor_tensor(z_lo[:, q % 2, :], f_tok[:, :, :].rearrange("p t d -> p (t d)"),
                                z_hi[:, q % 2, :].bitcast(F32),
                                ALU.subtract).then_inc(zlo_ready, 1)

            def split_w1(q):
                if q >= 2:
                    dve.wait_ge(hid_up, SLOTS * (q - 1))
                for k in range(TOP):
                    head = P if q == 0 and k == 0 else 0
                    if head:
                        dve.wait_ge(w1_head_hi, 1)
                        V.tensor_tensor(w1_lo[:, 0, 0, 0:head], w_sb[:, 0, 0, 0:head],
                                        w1_hi[:, 0, 0, 0:head].bitcast(F32), ALU.subtract).then_inc(w1_head_lo, 1)
                    dve.wait_ge(w1_hi_ready, TOP * q + k + 1)
                    V.tensor_tensor(w1_lo[:, q % 2, k, head:], w_sb[:, q % 2, k, head:F],
                                    w1_hi[:, q % 2, k, head:].bitcast(F32), ALU.subtract).then_inc(w1_lo_ready, 1)

            def widen_sum(q):
                dve.wait_ge(zt_ready, q + 1)
                if q:
                    dve.wait_ge(logits_up, q)
                V.tensor_scalar(zsum_wide[:, :], ones[:, :], zsum[:, 0:1], None, ALU.mult).then_inc(zwide_ready, 1)

            def route(q):
                dve.wait_ge(logits_read, q + 1)
                V.max(top_v[:, :], logit[:, :]).then_inc(top_ready, 1)
                dve.wait_ge(top_ready, q + 1)
                if q:
                    dve.wait_ge(w2_in[(q - 1) % 2], 16 * TOP * ((q - 1) // 2 + 1))
                V.max_index(top_i[:, :], top_v[:, :], logit[:, :]).then_inc(index_ready, 1)
                if q:
                    dve.wait_ge(tanh_ready, q)
                V.tensor_tensor(top_d[:, :], top_v[:, 0:1], top_v[:, 1:2], ALU.subtract).then_inc(diff_ready, 1)

            def coefficients(q):
                dve.wait_ge(tanh_ready, q + 1)
                for k in range(TOP):
                    V.tensor_scalar(coef[:, q % 2, k:k + 1], top_t[:, :], 0.25 if k == 0 else -0.25, 0.25,
                                    ALU.mult, ALU.add).then_inc(coef_ready, 1)

            def scale_w2(q):
                dve.wait_ge(w2_in[q % 2], 16 * TOP * (q // 2 + 1))
                dve.wait_ge(coef_ready, TOP * (q + 1))
                n = split_of(q) * P
                for k in range(TOP):
                    if n:
                        dve.wait_ge(w2_hi_ready, TOP * sum(split_of(p) > 0 for p in range(q)) + k + 1)
                        V.scalar_tensor_tensor(w2_lo[:, q % 2, k, 0:n], w_sb[:, q % 2, k, W2_AT:W2_AT + n],
                                               coef[:, q % 2, k:k + 1], w2_hi[:, q % 2, k, 0:n].bitcast(F32),
                                               ALU.mult, ALU.subtract).then_inc(w2_lo_ready, 1)
                    if n < F:
                        w2 = w_sb[:, q % 2, k, W2_AT + n:W2_AT + F]
                        V.tensor_scalar(w2, w2, coef[:, q % 2, k:k + 1], None, ALU.mult).then_inc(w2_scaled, 1)

            def split_hid(slot):
                dve.wait_ge(hid_hi_ready, split_slots(slot))
                if slot >= 2:
                    dve.wait_ge(hid_used, slot - 1)
                V.tensor_tensor(hid_lo[:, slot % 2, :], hid[:, slot % HBUF, :], hid_hi[:, slot % 2, :].bitcast(F32),
                                ALU.subtract).then_inc(hid_lo_ready, 1)

            def out_bias(q):
                dve.wait_ge(w2_in[q % 2], 16 * TOP * (q // 2 + 1))
                dve.wait_ge(coef_ready, TOP * (q + 1))
                b2 = [w_sb[:, q % 2, k, B2_AT:B2_AT + 1] for k in range(TOP)]
                V.tensor_scalar(bias2a[:, :], b2[0], coef[:, q % 2, 0:1], None, ALU.mult).then_inc(bias2a_ready, 1)
                dve.wait_ge(bias2a_ready, q + 1)
                V.scalar_tensor_tensor(bias2[:, q % 2, :], b2[1], coef[:, q % 2, 1:2], bias2a[:, :],
                                       ALU.mult, ALU.add).then_inc(bias2_ready, 1)

            def update_x(q):
                xb = xt[:, q % B, :, :].rearrange("p t d -> p (t d)")
                for half in range(2):
                    cols = slice(half * HALF, (half + 1) * HALF)
                    dve.wait_ge(y_turned, 2 * q + 1 + half)
                    V.tensor_tensor(xb[:, cols], aux_ps[:, cols], xb[:, cols], ALU.add).then_inc(x_updated, 1)

            def mixer_stats(b):
                dve.wait_ge(x_updated, 2 * (b + 1))
                for t in range(NT):
                    V.bn_stats(m_stat[:, t, :], xt[:, b, t, :]).then_inc(m_stats_step, 1)
                if b:
                    dve.wait_ge(m_pool_step, POOL_STEPS * b)
                for t in range(NT):
                    dve.wait_ge(m_stats_step, NT * b + t + 1)
                    V.bn_aggr(m_mv[:, t, :], m_stat[:, t, :]).then_inc(m_aggr_done, 1)

            def mixer_normalise(b):
                dve.wait_ge(m_pool_step, POOL_STEPS * b + 3)
                dve.wait_ge(m_aggr_done, NT * (b + 1))
                if b:
                    dve.wait_ge(m_turned, b)
                    dve.wait_ge(m_h_done, NT * b)
                for t in range(NT):
                    V.tensor_scalar(m_tok[:, t, :], xt[:, b, t, :], m_mv[:, t, 0:1], m_inv[:, 1, t:t + 1],
                                    ALU.subtract, ALU.mult).then_inc(m_norm_done, 1)

            def mixer_clip(b):
                dve.wait_ge(xs_ready, b + 1)
                V.tensor_scalar(xs[:, PAD:], xs[:, PAD:], XN_MAX, -XN_MAX, ALU.min, ALU.max).then_inc(xs_clipped, 1)

            def mixer_conv(b, k):
                dve.wait_ge(conv_step, 4 * b + k)
                V.scalar_tensor_tensor(xc[:, :], xs[:, k:k + N], conv_w[:, k:k + 1], xc[:, :],
                                       ALU.mult, ALU.add).then_inc(conv_step, 1)

            def mixer_silu(b):
                dve.wait_ge(silu_tanh, b + 1)
                V.scalar_tensor_tensor(silu[:, :], silu[:, :], 1.0, xc[:, :],
                                       ALU.add, ALU.mult).then_inc(silu_done, 1)

            def mixer_silu_lo(b):
                dve.wait_ge(silu_hi_done, b + 1)
                if b:
                    dve.wait_ge(gate_up, b)
                V.tensor_tensor(silu_lo[:, :], silu[:, :], silu_hi[:, :].bitcast(F32),
                                ALU.subtract).then_inc(silu_lo_done, 1)

            def mixer_decay(b):
                dve.wait_ge(dt_ln, b + 1)
                V.tensor_scalar(dt_t[:, :], dt_t[:, :], DT_MIN, DT_MAX, ALU.max, ALU.min).then_inc(dt_done, 1)
                dve.wait_ge(dt_done, b + 1)
                V.tensor_tensor_scan(decay[:, :], in_chunk[:, :], dt_t[:, :], 0.0,
                                     ALU.mult, ALU.add).then_inc(decay_sum, 1)

            def mixer_dstep(b):
                dve.wait_ge(decay_sum, b + 1)
                V.tensor_scalar(decay[:, :], decay[:, :], DECAY_MAX, None, ALU.min).then_inc(decay_done, 1)
                dve.wait_ge(decay_done, b + 1)
                if b:
                    dve.wait_ge(alpha_exp, b)
                V.tensor_tensor(dstep[:, 1:N], decay[:, 0:N - 1], decay[:, 1:N], ALU.subtract).then_inc(dstep_done, 1)

            def mixer_carry_decay(b):
                dve.wait_ge(decay_done, b + 1)
                if b:
                    dve.wait_ge(small_exp, b)
                V.tensor_scalar(small[:, 0, :], first_of(decay), -1.0, None, ALU.mult).then_inc(first_done, 1)
                V.tensor_tensor_scan(cumd[:, :], last_of(decay), cum_cap[:, :], 0.0,
                                     ALU.add, ALU.min).then_inc(cumd_done, 1)
                dve.wait_ge(cumd_done, b + 1)
                V.tensor_scalar(ncd[:, :], cumd[:, :], cumd[:, 0:1], DECAY_MAX,
                                ALU.subtract, ALU.min).then_inc(ncd_done, 1)
                dve.wait_ge(ncd_done, b + 1)
                V.tensor_tensor(small[:, 1, 1:NCH], ncd[:, 0:NCH - 1], ncd[:, 1:NCH],
                                ALU.subtract).then_inc(small_done, 1)

            def mixer_input(b):
                dve.wait_ge(v_sin, 2 * (b + 1))
                V.tensor_tensor(va[:, :], va[:, :], vb[:, :], ALU.add).then_inc(v_rot, 1)

            def mixer_times_dt(b):
                dve.wait_ge(dt_done, b + 1)
                dve.wait_ge(v_rot, b + 1)
                V.tensor_tensor(u[:, :], va[:, :], dt_t[:, :], ALU.mult).then_inc(u_ready, 1)

            def mixer_cos(b):
                for half in range(2):
                    cols = slice(half * HALF, (half + 1) * HALF)
                    dve.wait_ge(v_up, 2 * b + 1 + half)
                    V.tensor_tensor(va[:, cols], aux_ps[:, cols], rope_sb[:, 0, cols],
                                    ALU.mult).then_inc(v_cos, 1)

            def mixer_sin(b):
                for half in range(2):
                    cols = slice(half * HALF, (half + 1) * HALF)
                    dve.wait_ge(vs_up, 2 * b + 1 + half)
                    V.tensor_tensor(vb[:, cols], aux_ps[:, cols], rope_sb[:, 1, cols],
                                    ALU.mult).then_inc(v_sin, 1)

            def mixer_scan(b):
                dve.wait_ge(alpha_exp, b + 1)
                V.memset(first_of(alpha), 0.0).then_inc(alpha_done, 1)
                dve.wait_ge(alpha_done, b + 1)
                dve.wait_ge(u_ready, b + 1)
                if b:
                    dve.wait_ge(heads_up, 2 * b)
                V.tensor_tensor_scan(state[:, :], alpha[:, :], u[:, :], 0.0, ALU.mult, ALU.add).then_inc(local_done, 1)

            def mixer_scan2(b):
                dve.wait_ge(local_done, b + 1)
                dve.wait_ge(small_exp, b + 1)
                V.tensor_tensor_scan(carry[:, 1:NCH], last_of(state)[:, 0:NCH - 1], small_e[:, 1, 1:NCH], 0.0,
                                     ALU.add, ALU.mult).then_inc(carry_done, 1)
                dve.wait_ge(carry_done, b + 1)
                V.tensor_tensor(carry_p[:, 1:NCH], carry[:, 1:NCH], small_e[:, 0, 1:NCH],
                                ALU.mult).then_inc(carry_scaled, 1)
                dve.wait_ge(carry_scaled, b + 1)
                V.tensor_tensor(first_of(u)[:, 1:NCH], first_of(u)[:, 1:NCH], carry_p[:, 1:NCH],
                                ALU.add).then_inc(u_seeded, 1)
                dve.wait_ge(u_seeded, b + 1)
                V.tensor_tensor_scan(state[:, :], alpha[:, :], u[:, :], 0.0, ALU.mult, ALU.add).then_inc(final_done, 1)

            def mixer_gated(b):
                dve.wait_ge(gate_tanh, b + 1)
                for half in range(2):
                    cols = slice(half * HALF, (half + 1) * HALF)
                    dve.wait_ge(heads_up, 2 * b + 1 + half)
                    V.scalar_tensor_tensor(gated[:, cols], gated[:, cols], 1.0, aux_ps[:, cols],
                                           ALU.add, ALU.mult).then_inc(gated_done, 1)

            def mixer_add(b):
                dve.wait_ge(x_plus_h, b + 1)
                xb = xt[:, b, :, :].rearrange("p t d -> p (t d)")
                for half in range(2):
                    cols = slice(half * HALF, (half + 1) * HALF)
                    dve.wait_ge(out_up, 2 * b + 1 + half)
                    V.tensor_tensor(xb[:, cols], aux_ps[:, cols], xb[:, cols], ALU.add).then_inc(x_mixed, 1)

            def mixer_constants():
                dve.wait_ge(made_ident, 2)
                dve.wait_ge(vecs_in, 16)
                V.tensor_reduce(head_eye[:, :], ident[:, :].rearrange("p (h d) -> p d h", d=DH), AX_X,
                                ALU.add).then_inc(made_proj, 1)
                dve.wait_ge(made_proj, 2)
                V.tensor_tensor(mix_sb[:, :, :], head_eye[:, :].unsqueeze(1).broadcast_to([P, H, DH]),
                                mix_col.unsqueeze(2).broadcast_to([P, H, DH]), ALU.mult).then_inc(made_mix, 1)
                dve.wait_ge(proj_hi_ready, 1)
                V.tensor_tensor(proj_lo[:, :, :], proj_sb[:, 0:4, :], proj_hi[:, :, :].bitcast(F32),
                                ALU.subtract).then_inc(made_proj, 1)

            pass_stats(0)
            pass_normalise(0)
            dve.wait_ge(zwide_up, 1)
            V.tensor_copy(zsum_wide[:, :], y_ps[:, 0:P]).then_inc(zwide_ready, 1)
            route(0)
            pass_stats(1)
            split_z(0)
            coefficients(0)
            dve.wait_ge(proj_in, 16)
            flat = proj_sb[:, :, :].rearrange("p k n -> p (k n)")
            V.tensor_scalar(flat, flat, 0.5, None, ALU.mult).then_inc(made_proj, 1)
            split_w1(0)
            pass_normalise(1)
            scale_w2(0)
            dve.wait_ge(made_const, 8)
            dve.wait_ge(rope_in, 16)
            before, after = BEFORE["dve"], AFTER["dve"]
            for tick in range(LAST):
                for slot in split_at(tick, SLOT["lo"]):
                    split_hid(slot)
                if tick == 3 * TICKS + 1:
                    out_bias(0)
                    mixer_constants()
                for q in before_pass(tick, before["stats"], 2):
                    pass_stats(q)
                for q in before_pass(tick, before["normalise"], 2):
                    pass_normalise(q)
                for q in after_pass(tick, after["update"]):
                    update_x(q)
                for b in mixer_at(tick, after["stats"]):
                    mixer_stats(b)
                for q in before_pass(tick, before["widen"]):
                    widen_sum(q)
                for q in before_pass(tick, before["split_z"]):
                    split_z(q)
                for q in before_pass(tick, before["route"]):
                    route(q)
                for q in before_pass(tick, before["coef"]):
                    coefficients(q)
                for q in before_pass(tick, before["split_w1"]):
                    split_w1(q)
                for q in before_pass(tick, before["scale_w2"]):
                    scale_w2(q)
                for q in before_pass(tick, before["bias"]):
                    out_bias(q)
                for b in mixer_at(tick, after["normalise"]):
                    mixer_normalise(b)
                for b in mixer_at(tick, after["clip"]):
                    mixer_clip(b)
                for k in range(1, 4):
                    for b in mixer_at(tick, after[f"conv{k}"]):
                        mixer_conv(b, k)
                for b in mixer_at(tick, after["silu"]):
                    mixer_silu(b)
                for b in mixer_at(tick, after["silu_lo"]):
                    mixer_silu_lo(b)
                for b in mixer_at(tick, after["cos"]):
                    mixer_cos(b)
                for b in mixer_at(tick, after["sin"]):
                    mixer_sin(b)
                for b in mixer_at(tick, after["decay"]):
                    mixer_decay(b)
                for b in mixer_at(tick, after["dstep"]):
                    mixer_dstep(b)
                for b in mixer_at(tick, after["carry"]):
                    mixer_carry_decay(b)
                for b in mixer_at(tick, after["u"]):
                    mixer_input(b)
                for b in mixer_at(tick, after["u2"]):
                    mixer_times_dt(b)
                for b in mixer_at(tick, after["scan"]):
                    mixer_scan(b)
                for b in mixer_at(tick, after["scan2"]):
                    mixer_scan2(b)
                for b in mixer_at(tick, after["gated"]):
                    mixer_gated(b)
                for b in mixer_at(tick, after["add"]):
                    mixer_add(b)


def kernel(L0_attn_x, L0_attn_norm_scale, L0_attn_conv_w, L0_attn_conv_b, L0_attn_in_proj_w, L0_attn_dt_bias,
           L0_attn_head_mix, L0_attn_out_proj_w, L0_ffn_gate_w, L0_ffn_w1, L0_ffn_b1, L0_ffn_w2, L0_ffn_b2):
    import numpy as np
    import concourse.bacc as bacc
    from concourse.bass_utils import run_bass_kernel_spmd

    def arr(a):
        return np.ascontiguousarray(np.asarray(a))

    x = arr(L0_attn_x)
    B, N, D = x.shape
    H = L0_attn_head_mix.shape[0]
    dh = D // H
    E, _, F = L0_ffn_w1.shape
    ft = F // D
    w2 = arr(L0_ffn_w2).reshape(E, ft, D, D).transpose(0, 2, 1, 3).reshape(E, D, F)
    b1 = arr(L0_ffn_b1).reshape(E, ft, D).transpose(0, 2, 1)
    b2 = arr(L0_ffn_b2)[:, :, None]
    wpack = np.concatenate([arr(L0_ffn_w1), b1, w2, b2], axis=2)
    win = arr(L0_attn_in_proj_w)
    swapped = win[:, D:2 * D].reshape(D, H, 2, dh // 2)[:, :, ::-1, :].reshape(D, D)
    proj = np.concatenate([win[:, :2 * D], swapped, win[:, 2 * D:], arr(L0_attn_out_proj_w)], axis=1)
    vecs = np.concatenate([arr(L0_attn_conv_w).reshape(D, -1), arr(L0_attn_conv_b)[:, None],
                           arr(L0_attn_dt_bias)[:, None], arr(L0_attn_norm_scale)[:, None],
                           np.repeat(arr(L0_attn_head_mix), dh, axis=0)], axis=1)
    inv = (1.0 / np.float32(10000.0) ** (np.arange(0, dh, 2, dtype=np.float32) / np.float32(dh))).astype(np.float32)
    ang = (np.arange(N, dtype=np.float32)[None, :] * inv[:, None]).astype(np.float32).astype(np.float64)
    cos, sin = np.cos(ang), np.sin(ang)
    rope = np.stack([np.tile(np.concatenate([cos, cos]), (H, 1)),
                     np.tile(np.concatenate([-sin, sin]), (H, 1))]).astype(np.float32)

    ins = {"x_dram": x, "wpack_dram": wpack, "gate_w_dram": arr(L0_ffn_gate_w), "proj_dram": proj,
           "vecs_dram": vecs, "rope_dram": rope}
    from concourse import mybir as mb
    nc = bacc.Bacc("TRN2", target_bir_lowering=False, num_devices=1)
    aps = []
    for name in list(ins):
        a = ins[name] = np.ascontiguousarray(ins[name])
        aps.append(nc.dram_tensor(name, a.shape, mb.dt.from_np(a.dtype), kind="ExternalInput").ap())
    res = nc.dram_tensor("out_dram", x.shape, mb.dt.float32, kind="ExternalOutput").ap()
    macaron_kernel(nc, *aps, res)
    r = run_bass_kernel_spmd(nc, [ins], core_ids=[0])
    return r.results[0]["out_dram"]
```
